# Optimizing a Trainium2 kernel written in Bass

```python
import numpy as np
import jax
import jax.numpy as jnp

def _softmax(x, axis=-1):
    return jax.nn.softmax(x, axis=axis)

def _gelu(x):
    return jax.nn.gelu(x, approximate=True)

def _silu(x):
    return jax.nn.silu(x)

def _sigmoid(x):
    return jax.nn.sigmoid(x)

def _layernorm(x, axis=-1, eps=1e-05):
    m = jnp.mean(x, axis=axis, keepdims=True)
    v = jnp.var(x, axis=axis, keepdims=True)
    return (x - m) / jnp.sqrt(v + eps)

def _scatter_add(tgt, idx, src, axis=0):
    return tgt.at[idx].add(src)

def _segment_sum(src, seg, n):
    return jax.ops.segment_sum(src, seg, n)
kernel_name = 'mk_conv_seq_d4_conv_nchw512_r2_e73aa4'

def setup_inputs(seed: int=0):
    np.random.seed(seed)
    _w = jnp.asarray

    def _rec_inputs():
        import jax
        import jax.numpy as jnp
        _gk = jax.random.key(seed)
        x = 7.22e-05 + 1 * jax.random.normal(jax.random.fold_in(_gk, 1), (4, 256, 32, 32), jnp.float32)
        return x
    x = _rec_inputs()

    def _L0_conv_setup():
        import jax, jax.numpy as jnp
        import numpy as np
        B, C, H, W = (4, 256, 32, 32)
        C8 = C // 8
        EPS = 1e-05
        key = jax.random.key(seed)
        ks = jax.random.split(key, 8)
        s_in = 1.0 / np.sqrt(C)
        return {'x': jax.random.normal(ks[0], (B, C, H, W), jnp.float32), 'Wq': jax.random.normal(ks[1], (C8, C), jnp.float32) * s_in, 'bq': jnp.zeros((C8,), jnp.float32), 'Wk': jax.random.normal(ks[2], (C8, C), jnp.float32) * s_in, 'bk': jnp.zeros((C8,), jnp.float32), 'Wv': jax.random.normal(ks[3], (C, C), jnp.float32) * s_in, 'bv': jnp.zeros((C,), jnp.float32), 'gamma': jnp.asarray(0.1, jnp.float32), 'bn_w': jnp.ones((C,), jnp.float32), 'bn_b': jnp.zeros((C,), jnp.float32)}
    _L0_conv_all = _L0_conv_setup()
    _L0_conv_in = {k: v for k, v in _L0_conv_all.items() if k in ('Wq', 'bq', 'Wk', 'bk', 'Wv', 'bv', 'gamma', 'bn_w', 'bn_b')}
    del _L0_conv_all

    def _L1_conv_setup():
        import jax, jax.numpy as jnp
        import numpy as np
        import math
        C = 256
        G = 32
        EPS = 1e-05

        def _group_norm(x, gamma, beta):
            b, c, h, w = x.shape
            xg = x.reshape(b, G, c // G * h * w)
            mu = jnp.mean(xg, axis=-1, keepdims=True)
            var = jnp.var(xg, axis=-1, keepdims=True)
            xn = ((xg - mu) / jnp.sqrt(var + EPS)).reshape(b, c, h, w)
            return xn * gamma[None, :, None, None] + beta[None, :, None, None]
        key = jax.random.key(seed)
        ks = jax.random.split(key, 7)
        B, H, W = (16, 32, 32)
        x = jax.random.normal(ks[0], (B, C, H, W), dtype=jnp.float32)
        gamma = jnp.ones((C,), dtype=jnp.float32)
        beta = jnp.zeros((C,), dtype=jnp.float32)
        fan = 1.0 / math.sqrt(C)
        qkv_w = jax.random.uniform(ks[1], (3 * C, C), minval=-fan, maxval=fan, dtype=jnp.float32)
        qkv_b = jax.random.uniform(ks[2], (3 * C,), minval=-fan, maxval=fan, dtype=jnp.float32)
        proj_w = jax.random.uniform(ks[3], (C, C), minval=-fan, maxval=fan, dtype=jnp.float32)
        proj_b = jax.random.uniform(ks[4], (C,), minval=-fan, maxval=fan, dtype=jnp.float32)
        return {'x': x, 'gamma': gamma, 'beta': beta, 'qkv_w': qkv_w, 'qkv_b': qkv_b, 'proj_w': proj_w, 'proj_b': proj_b}
    _L1_conv_all = _L1_conv_setup()
    _L1_conv_in = {k: v for k, v in _L1_conv_all.items() if k in ('gamma', 'beta', 'qkv_w', 'qkv_b', 'proj_w', 'proj_b')}
    del _L1_conv_all

    def _L2_conv_setup():
        import jax, jax.numpy as jnp
        import numpy as np
        import math
        C = 256
        N_HEADS = 8
        N_GROUPS = 32
        EPS = 1e-05
        key = jax.random.key(seed)
        k1, k2, k3 = jax.random.split(key, 3)
        B, H, W = (4, 48, 48)
        x = jax.random.normal(k1, (B, C, H, W), dtype=jnp.float32)
        gn_w = jnp.ones((C,), jnp.float32)
        gn_b = jnp.zeros((C,), jnp.float32)
        qkv_w = jax.random.normal(k2, (3 * C, C), jnp.float32) * (1.0 / math.sqrt(C))
        qkv_b = jnp.zeros((3 * C,), jnp.float32)
        proj_w = jax.random.normal(k3, (C, C), jnp.float32) * (1.0 / math.sqrt(C))
        proj_b = jnp.zeros((C,), jnp.float32)
        return {'x': x, 'gn_w': gn_w, 'gn_b': gn_b, 'qkv_w': qkv_w, 'qkv_b': qkv_b, 'proj_w': proj_w, 'proj_b': proj_b}
    _L2_conv_all = _L2_conv_setup()
    _L2_conv_in = {k: v for k, v in _L2_conv_all.items() if k in ('gn_w', 'gn_b', 'qkv_w', 'qkv_b', 'proj_w', 'proj_b')}
    del _L2_conv_all

    def _L3_conv_setup():
        import jax, jax.numpy as jnp
        import numpy as np
        GROUPS = 32
        N_HEADS = 8
        EPS = 1e-05
        key = jax.random.key(seed)
        ks = jax.random.split(key, 4)
        B, C, H, W = (8, 256, 32, 32)
        x = jax.random.normal(ks[0], (B, C, H, W), dtype=jnp.float32)
        norm_scale = jnp.ones((C,), jnp.float32)
        norm_bias = jnp.zeros((C,), jnp.float32)
        qkv_w = jax.random.normal(ks[1], (3 * C, C), jnp.float32) * C ** (-0.5)
        qkv_b = jnp.zeros((3 * C,), jnp.float32)
        proj_w = jax.random.normal(ks[2], (C, C), jnp.float32) * C ** (-0.5)
        proj_b = jnp.zeros((C,), jnp.float32)
        return {'x': x, 'norm_scale': norm_scale, 'norm_bias': norm_bias, 'qkv_w': qkv_w, 'qkv_b': qkv_b, 'proj_w': proj_w, 'proj_b': proj_b}
    _L3_conv_all = _L3_conv_setup()
    _L3_conv_in = {k: v for k, v in _L3_conv_all.items() if k in ('norm_scale', 'norm_bias', 'qkv_w', 'qkv_b', 'proj_w', 'proj_b')}
    del _L3_conv_all
    return {'x': x, 'L0_conv_Wq': _L0_conv_in['Wq'], 'L0_conv_bq': _L0_conv_in['bq'], 'L0_conv_Wk': _L0_conv_in['Wk'], 'L0_conv_bk': _L0_conv_in['bk'], 'L0_conv_Wv': _L0_conv_in['Wv'], 'L0_conv_bv': _L0_conv_in['bv'], 'L0_conv_gamma': _L0_conv_in['gamma'], 'L0_conv_bn_w': _L0_conv_in['bn_w'], 'L0_conv_bn_b': _L0_conv_in['bn_b'], 'L1_conv_gamma': _L1_conv_in['gamma'], 'L1_conv_beta': _L1_conv_in['beta'], 'L1_conv_qkv_w': _L1_conv_in['qkv_w'], 'L1_conv_qkv_b': _L1_conv_in['qkv_b'], 'L1_conv_proj_w': _L1_conv_in['proj_w'], 'L1_conv_proj_b': _L1_conv_in['proj_b'], 'L2_conv_gn_w': _L2_conv_in['gn_w'], 'L2_conv_gn_b': _L2_conv_in['gn_b'], 'L2_conv_qkv_w': _L2_conv_in['qkv_w'], 'L2_conv_qkv_b': _L2_conv_in['qkv_b'], 'L2_conv_proj_w': _L2_conv_in['proj_w'], 'L2_conv_proj_b': _L2_conv_in['proj_b'], 'L3_conv_norm_scale': _L3_conv_in['norm_scale'], 'L3_conv_norm_bias': _L3_conv_in['norm_bias'], 'L3_conv_qkv_w': _L3_conv_in['qkv_w'], 'L3_conv_qkv_b': _L3_conv_in['qkv_b'], 'L3_conv_proj_w': _L3_conv_in['proj_w'], 'L3_conv_proj_b': _L3_conv_in['proj_b']}

def reference(x, L0_conv_Wq, L0_conv_bq, L0_conv_Wk, L0_conv_bk, L0_conv_Wv, L0_conv_bv, L0_conv_gamma, L0_conv_bn_w, L0_conv_bn_b, L1_conv_gamma, L1_conv_beta, L1_conv_qkv_w, L1_conv_qkv_b, L1_conv_proj_w, L1_conv_proj_b, L2_conv_gn_w, L2_conv_gn_b, L2_conv_qkv_w, L2_conv_qkv_b, L2_conv_proj_w, L2_conv_proj_b, L3_conv_norm_scale, L3_conv_norm_bias, L3_conv_qkv_w, L3_conv_qkv_b, L3_conv_proj_w, L3_conv_proj_b):
    import jax
    import jax.numpy as jnp

    def _L0_conv_ref(x, Wq, bq, Wk, bk, Wv, bv, gamma, bn_w, bn_b):
        import jax, jax.numpy as jnp
        import numpy as np
        B, C, H, W = (4, 256, 32, 32)
        C8 = C // 8
        EPS = 1e-05
        b, c, h, w = x.shape
        n = h * w
        xf = x.reshape(b, c, n)
        q = jnp.einsum('kc,bcn->bkn', Wq, xf) + bq[None, :, None]
        k = jnp.einsum('kc,bcn->bkn', Wk, xf) + bk[None, :, None]
        v = jnp.einsum('dc,bcn->bdn', Wv, xf) + bv[None, :, None]
        energy = jnp.einsum('bki,bkj->bij', q, k)
        attn = jax.nn.softmax(energy, axis=-1)
        out = jnp.einsum('bcj,bij->bci', v, attn).reshape(b, c, h, w)
        out = gamma * out + x
        mean = jnp.mean(out, axis=(0, 2, 3), keepdims=True)
        var = jnp.var(out, axis=(0, 2, 3), keepdims=True)
        out = (out - mean) * jax.lax.rsqrt(var + EPS)
        out = out * bn_w[None, :, None, None] + bn_b[None, :, None, None]
        return out

    def _L1_conv_ref(x, gamma, beta, qkv_w, qkv_b, proj_w, proj_b):
        import jax, jax.numpy as jnp
        import numpy as np
        import math
        C = 256
        G = 32
        EPS = 1e-05

        def _group_norm(x, gamma, beta):
            b, c, h, w = x.shape
            xg = x.reshape(b, G, c // G * h * w)
            mu = jnp.mean(xg, axis=-1, keepdims=True)
            var = jnp.var(xg, axis=-1, keepdims=True)
            xn = ((xg - mu) / jnp.sqrt(var + EPS)).reshape(b, c, h, w)
            return xn * gamma[None, :, None, None] + beta[None, :, None, None]
        b, c, h, w = x.shape
        hn = _group_norm(x, gamma, beta)
        qkv = jnp.einsum('bchw,oc->bohw', hn, qkv_w) + qkv_b[None, :, None, None]
        q, k, v = jnp.split(qkv, 3, axis=1)
        q = q.reshape(b, c, h * w).transpose(0, 2, 1)
        k = k.reshape(b, c, h * w).transpose(0, 2, 1)
        v = v.reshape(b, c, h * w).transpose(0, 2, 1)
        scale = 1.0 / math.sqrt(c)
        attn = jax.nn.softmax(jnp.einsum('bnc,bmc->bnm', q, k) * scale, axis=-1)
        out = jnp.einsum('bnm,bmc->bnc', attn, v)
        out = out.transpose(0, 2, 1).reshape(b, c, h, w)
        out = jnp.einsum('bchw,oc->bohw', out, proj_w) + proj_b[None, :, None, None]
        return x + out

    def _L2_conv_ref(x, gn_w, gn_b, qkv_w, qkv_b, proj_w, proj_b):
        import jax, jax.numpy as jnp
        import numpy as np
        import math
        C = 256
        N_HEADS = 8
        N_GROUPS = 32
        EPS = 1e-05
        b, c, h, w = x.shape
        T = h * w
        xf = x.reshape(b, c, T)
        xg = xf.reshape(b, N_GROUPS, c // N_GROUPS, T)
        mean = xg.mean(axis=(2, 3), keepdims=True)
        var = xg.var(axis=(2, 3), keepdims=True)
        xn = (xg - mean) * jax.lax.rsqrt(var + EPS)
        xn = xn.reshape(b, c, T) * gn_w[None, :, None] + gn_b[None, :, None]
        qkv = jnp.einsum('oc,bct->bot', qkv_w, xn) + qkv_b[None, :, None]
        ch = c // N_HEADS
        qkv = qkv.reshape(b * N_HEADS, 3 * ch, T)
        q, k, v = jnp.split(qkv, 3, axis=1)
        scale = 1.0 / math.sqrt(math.sqrt(ch))
        weight = jnp.einsum('bct,bcs->bts', q * scale, k * scale)
        weight = jax.nn.softmax(weight.astype(jnp.float32), axis=-1).astype(qkv.dtype)
        a = jnp.einsum('bts,bcs->bct', weight, v).reshape(b, c, T)
        hout = jnp.einsum('oc,bct->bot', proj_w, a) + proj_b[None, :, None]
        return (xn + hout).reshape(b, c, h, w)

    def _L3_conv_ref(x, norm_scale, norm_bias, qkv_w, qkv_b, proj_w, proj_b):
        import jax, jax.numpy as jnp
        import numpy as np
        GROUPS = 32
        N_HEADS = 8
        EPS = 1e-05
        B, C, H, W = x.shape
        T = H * W
        xf = x.reshape(B, C, T)
        xg = xf.astype(jnp.float32).reshape(B, GROUPS, C // GROUPS, T)
        mean = xg.mean(axis=(2, 3), keepdims=True)
        var = xg.var(axis=(2, 3), keepdims=True)
        xn = ((xg - mean) * jax.lax.rsqrt(var + EPS)).reshape(B, C, T)
        xn = (xn * norm_scale[:, None] + norm_bias[:, None]).astype(x.dtype)
        qkv = jnp.einsum('oc,bct->bot', qkv_w, xn) + qkv_b[:, None]
        ch = C // N_HEADS
        qkv_h = qkv.reshape(B * N_HEADS, 3 * ch, T)
        q, k, v = (qkv_h[:, :ch], qkv_h[:, ch:2 * ch], qkv_h[:, 2 * ch:])
        scale = ch ** (-0.25)
        weight = jnp.einsum('bct,bcs->bts', q * scale, k * scale)
        weight = jax.nn.softmax(weight.astype(jnp.float32), axis=-1).astype(qkv.dtype)
        a = jnp.einsum('bts,bcs->bct', weight, v).reshape(B, C, T)
        h = jnp.einsum('oc,bct->bot', proj_w, a) + proj_b[:, None]
        return (xf + h).reshape(B, C, H, W)

    def _gn(v, G=32, eps=1e-05):
        B_, C_, H_, W_ = v.shape
        g = v.reshape(B_, G, C_ // G, H_, W_)
        m = jnp.mean(g, axis=(2, 3, 4), keepdims=True)
        s = jnp.var(g, axis=(2, 3, 4), keepdims=True)
        return ((g - m) / jnp.sqrt(s + eps)).reshape(v.shape)

    def _ln_c(v, eps=1e-06):
        m = jnp.mean(v, axis=1, keepdims=True)
        s = jnp.var(v, axis=1, keepdims=True)
        return (v - m) / jnp.sqrt(s + eps)

    def _ln_t(v, eps=1e-05):
        m = jnp.mean(v, axis=-1, keepdims=True)
        s = jnp.var(v, axis=-1, keepdims=True)
        return (v - m) / jnp.sqrt(s + eps)

    def _to_tokens(v):
        B_, C_, H_, W_ = v.shape
        return v.reshape(B_, C_, H_ * W_).transpose(0, 2, 1)

    def _from_tokens(t, like):
        B_, C_, H_, W_ = like.shape
        return t.transpose(0, 2, 1).reshape(B_, C_, H_, W_)
    x = _L0_conv_ref(x, L0_conv_Wq, L0_conv_bq, L0_conv_Wk, L0_conv_bk, L0_conv_Wv, L0_conv_bv, L0_conv_gamma, L0_conv_bn_w, L0_conv_bn_b)
    x = _L1_conv_ref(x, L1_conv_gamma, L1_conv_beta, L1_conv_qkv_w, L1_conv_qkv_b, L1_conv_proj_w, L1_conv_proj_b)
    x = _L2_conv_ref(x, L2_conv_gn_w, L2_conv_gn_b, L2_conv_qkv_w, L2_conv_qkv_b, L2_conv_proj_w, L2_conv_proj_b)
    x = _L3_conv_ref(x, L3_conv_norm_scale, L3_conv_norm_bias, L3_conv_qkv_w, L3_conv_qkv_b, L3_conv_proj_w, L3_conv_proj_b)
    return x

_drawn_inputs = setup_inputs


def setup_inputs(seed=0):
    import zlib

    import numpy as np

    out = dict(_drawn_inputs(seed))
    spreads = {'L0_conv_bq': (0.0, 0.491),
     'L0_conv_bk': (0.0, 0.8),
     'L0_conv_bv': (0.0, 0.8),
     'L0_conv_bn_w': (1.0, 0.2),
     'L0_conv_bn_b': (0.0, 0.1),
     'L1_conv_gamma': (1.0, 0.6),
     'L1_conv_beta': (0.0, 0.1),
     'L2_conv_gn_w': (1.0, 0.2),
     'L2_conv_gn_b': (0.0, 0.1),
     'L2_conv_qkv_b': (0.0, 0.1),
     'L2_conv_proj_b': (0.0, 0.1),
     'L3_conv_norm_scale': (1.0, 0.2),
     'L3_conv_norm_bias': (0.0, 0.1),
     'L3_conv_qkv_b': (0.0, 0.1),
     'L3_conv_proj_b': (0.0, 0.1)}
    factors = {}
    for name, (base, spread) in spreads.items():
        noise = np.random.default_rng([zlib.crc32(name.encode()), seed]).standard_normal(out[name].shape)
        drawn = base * np.exp(spread * noise) if base else spread * noise
        out[name] = jnp.asarray(drawn.astype(out[name].dtype))
    for name, factor in factors.items():
        out[name] = (out[name] * factor).astype(out[name].dtype)
    return out
```

```python
from contextlib import ExitStack

import concourse.bass as bass
from concourse import mybir

ALU = mybir.AluOpType
ACT = mybir.ActivationFunctionType
AX = mybir.AxisListType
F32 = mybir.dt.float32
F32R = mybir.dt.float32r

B, C, N = 4, 256, 1024
PART = 128
CT = C // PART
NT = N // PART
HALF = N // 2
HEADS, CH = 8, 32
QUADH = 4
GROUPS = HEADS // QUADH
K0 = C // 8
STACK = 3 * CH
EPS = 1e-5

STEPS = 2 * NT * QUADH
DIRECT = 3
ADDS = NT - DIRECT - 1
DMAS = QUADH * 6

PC = {"gamma0": 0, "bnw": 1, "bnb": 3, "bqk0": 5}
for _n, _l in enumerate((1, 2, 3)):
    for _k, _f in enumerate(("gw", "gb", "bp")):
        PC[f"{_f}{_l}"] = 6 + 10 * _n + 2 * _k
    PC[f"bqk{_l}"] = 12 + 10 * _n
NPAR = 36


def attention_stack(nc, x, w0, w1, w2, w3, wp1, wp2, wp3, bv0, bv1, bv2, bv3, par_d, ident_d, gmat_d, out):
    with ExitStack() as ctx:
        def sb(name, shape, dt=F32):
            return ctx.enter_context(nc.sbuf_tensor(name, shape, dt))

        def sem(name):
            return ctx.enter_context(nc.semaphore(name))

        X = sb("X", [PART, B, CT, N])
        XH = sb("XH", [PART, CT, N], F32R)
        XL = sb("XL", [PART, CT, N], F32R)
        SH = sb("SH", [PART, 2, N])
        SL = sb("SL", [PART, 2, N])
        KS = sb("KS", [PART, 2, QUADH, N], F32R)
        QS = sb("QS", [PART, 2, QUADH, N], F32R)
        V = sb("V", [PART, GROUPS, NT, PART])
        PR = sb("PR", [PART, 4, QUADH * HALF])
        PA = sb("PA", [PART, QUADH * HALF])
        A = sb("A", [PART, CT, N])
        RD = sb("RD", [PART, HALF])
        WH = sb("WH", [PART, CT, 3 * C], F32R)
        WL = sb("WL", [PART, CT, 3 * C], F32R)
        WP = sb("WP", [PART, CT, C])
        BV = sb("BV", [PART, C])
        PAR = sb("PAR", [PART, NPAR])
        ident = sb("identity", [PART, PART])
        gmat = sb("group_mean", [PART, PART])
        ones = sb("ones", [PART, PART])
        MX = sb("MX", [PART, 32])
        MROW = sb("MROW", [32, PART], F32R)
        BST = sb("BST", [PART, CT, 2, 6])
        MV = sb("MV", [PART, CT, 2])
        GST = sb("GST", [PART, CT, 2])
        VAR = sb("VAR", [PART, CT])
        RSTD = sb("RSTD", [PART, CT])
        MH = sb("MH", [PART, CT])
        SC = sb("SC", [PART, B, CT, 2])
        BNS = sb("BNS", [PART, CT, B * 2, 6])
        TMP = sb("TMP", [PART, CT])
        ONER = sb("ONER", [1, PART], F32R)
        MR1 = QS[0:1, 1, 0, :]

        psD = ctx.enter_context(nc.psum_tensor("psD", [PART, 2, N], F32))
        psA = ctx.enter_context(nc.psum_tensor("psA", [PART, 2, HALF], F32))
        psO = ctx.enter_context(nc.psum_tensor("psO", [PART, 2, HALF], F32))

        def par(name, n=1, p=PART):
            return PAR[0:p, PC[name]:PC[name] + n]


        x_v = x.rearrange("b (t p) n -> p b t n", p=PART)
        out_v = out.rearrange("b (t p) n -> p b t n", p=PART)
        w_dram = [w.rearrange("(t p) n -> p t n", p=PART) for w in (w0, w1, w2, w3)]
        wp_dram = [None] + [w.rearrange("(t p) n -> p t n", p=PART) for w in (wp1, wp2, wp3)]
        bv_dram = [bv0, bv1, bv2, bv3]

        s_x, s_const, s_memset = sem("x_loaded"), sem("constants_loaded"), sem("memsets_done")
        with nc.Block() as block:
            @block.sync
            def _(e):
                for tile, d in ((PAR, par_d), (ident, ident_d), (gmat, gmat_d)):
                    e.dma_start(tile[:, :], d).then_inc(s_const, 16)
                for b in range(B):
                    e.dma_start(X[:, b], x_v[:, b]).then_inc(s_x, 16)

            @block.vector
            def _(e):
                e.memset(ones[:, :], 1.0).then_inc(s_memset, 1)
                e.memset(MH[:, :], -0.5).then_inc(s_memset, 1)
                e.memset(KS[STACK:STACK + 1].bitcast(F32), 1.0).then_inc(s_memset, 1)
                e.memset(ONER[:, :].bitcast(F32), 1.0).then_inc(s_memset, 1)
                e.wait_ge(s_memset, 4)
                e.wait_ge(s_x, 16 * B)
                e.wait_ge(s_const, 48)

        def load_weights(layer, wide):
            s_w, s_wh, s_wl = sem(f"w_loaded{layer}"), sem(f"w_high{layer}"), sem(f"w_low{layer}")
            n = 2 if layer == 0 else 3
            raw = SL[:, :, :].rearrange("p t n -> p (t n)")[:, 0:CT * wide].rearrange("p (t n) -> p t n", t=CT)
            with nc.Block() as block:
                @block.sync
                def _(e):
                    e.dma_start(raw, w_dram[layer]).then_inc(s_w, 16)
                    e.dma_start(BV[:, :], bv_dram[layer]).then_inc(s_w, 16)
                    if layer:
                        e.dma_start(WP[:, :, :], wp_dram[layer]).then_inc(s_w, 16)

                @block.vector
                def _(e):
                    if layer == 2:
                        e.memset(KS[STACK:STACK + 1].bitcast(F32), 1.0)
                    e.wait_ge(s_w, 16 * n)
                    e.tensor_copy(WH[:, :, 0:wide], raw).then_inc(s_wh, 1)
                    e.wait_ge(s_wh, 1)
                    e.tensor_tensor(WL[:, :, 0:wide], raw, WH[:, :, 0:wide], ALU.subtract).then_inc(s_wl, 1)
                    e.wait_ge(s_wl, 1)

        def split_products(e, out_ap, terms):
            last = None
            for i, (w, m) in enumerate(terms):
                last = e.matmul(out_ap, w, m, start=(i == 0), stop=(i == len(terms) - 1))
            return last

        def project_in(e, slot, col, width):
            for h in range(2):
                mv = slice(h * HALF, (h + 1) * HALF)
                terms = [(w[:, t, col:col + width], xx[:, t, mv])
                         for w, xx in ((WH, XH), (WL, XH), (WH, XL)) for t in range(CT)]
                last = split_products(e, psD[0:width, slot, mv], terms)
            return last

        def project_values(e, slot, col):
            for n in range(NT):
                st = slice(n * PART, (n + 1) * PART)
                terms = [(xx[:, t, st], w[:, t, col:col + PART])
                         for xx, w in ((XH, WH), (XL, WH), (XH, WL)) for t in range(CT)]
                last = split_products(e, psD[:, slot, st], terms)
            return last

        def project_out(e, slot, o):
            for h in range(2):
                mv = slice(h * HALF, (h + 1) * HALF)
                last = split_products(e, psD[:, slot, mv],
                                      [(WP[:, t, o * PART:(o + 1) * PART], A[:, t, mv]) for t in range(CT)])
            return last

        def bias_values(e, slot, g):
            return e.tensor_tensor(V[:, g, :, :], psD[:, slot, :].rearrange("p (t c) -> p t c", t=NT),
                                   BV[:, g * PART:(g + 1) * PART].unsqueeze(1).broadcast_to((PART, NT, PART)),
                                   ALU.add)

        def norm_statistics(e, xb):
            for t in range(CT):
                for h in range(2):
                    e.bn_stats(BST[:, t, h, :], xb[:, t, h * HALF:(h + 1) * HALF])
            e.drain()
            for t in range(CT):
                e.bn_aggr(MV[:, t, :], BST[:, t, :, :].rearrange("p a b -> p (a b)"))
            e.drain()
            e.tensor_tensor(GST[:, :, 1], MV[:, :, 0], MV[:, :, 0], ALU.mult)
            e.drain()
            e.tensor_tensor(GST[:, :, 1], GST[:, :, 1], MV[:, :, 1], ALU.add)
            return e.tensor_copy(GST[:, :, 0], MV[:, :, 0])

        def group_variance(e):
            e.drain()
            e.tensor_tensor(TMP[:, :], MV[:, :, 0], MV[:, :, 0], ALU.mult)
            e.drain()
            e.tensor_tensor(TMP[:, :], MV[:, :, 1], TMP[:, :], ALU.subtract)
            e.drain()
            return e.tensor_scalar(VAR[:, :], TMP[:, :], EPS, None, ALU.add)

        def norm_factors(e, b, gw, gb):
            e.tensor_tensor(SC[:, b, :, 0], RSTD[:, :], par(gw, 2), ALU.mult)
            e.drain()
            e.tensor_tensor(TMP[:, :], MV[:, :, 0], SC[:, b, :, 0], ALU.mult)
            e.drain()
            e.tensor_tensor(SC[:, b, :, 1], par(gb, 2), TMP[:, :], ALU.subtract)
            e.drain()

        def single_head(layer):
            wide = (2 * K0 if layer == 0 else 2 * C) + C
            load_weights(layer, wide)
            L1 = layer == 1
            vcol = wide - C
            scale = 1.0 if layer == 0 else C ** -0.5
            units = (["s", "k0", "k1", "q0", "q1"] if L1 else ["qk"]) + ["v0", "v1"]
            units += ["m"] * NT + ["T", "d0", "d1"] + (["p0", "p1"] if L1 else [])
            ND = len(units)
            NQK = 4 if L1 else 1
            at = {u: i for i, u in enumerate(units)}
            first_m = units.index("m")
            KH, KL, QH, QL = KS[:, 0, 0:2], KS[:, 0, 2:4], QS[:, 0, 0:2], QS[:, 0, 2:4]
            n = f"_{layer}"
            d_full, d_free = sem("unit_full" + n), sem("unit_free" + n)
            st_full, exp_done = sem("scores_full" + n), sem("exp_done" + n)
            av_done, sum_done, out_done = sem("av_done" + n), sem("sum_done" + n), sem("out_done" + n)
            stat_done, var_done, rstd_done = sem("stat_done" + n), sem("var_done" + n), sem("rstd_done" + n)
            xn_done, xh_done, xl_done = sem("xn_done" + n), sem("xh_done" + n), sem("xl_done" + n)
            hi_done, lo_done = sem("qk_high" + n), sem("qk_low" + n)
            stack_dma, row_dma = sem("stack_filled" + n), sem("max_row_filled" + n)
            NSTACK = 6

            def units_freed(b, i):
                return b * ND + i + 3

            with nc.Block() as block:
                @block.tensor
                def _(e):
                    with e.Fori(0, B) as b:
                        def unit(i):
                            e.wait_ge(d_free, b * ND + i + 1)
                            u, slot = units[i], i % 2
                            if u == "s":
                                e.wait_ge(stat_done, b + 1)
                                mm = e.matmul(psD[:, slot, 0:4], gmat[:, :], GST[:, :, :].rearrange("p a b -> p (a b)"),
                                              start=True, stop=True)
                            elif u[0] in "kq":
                                if u in ("k0", "qk"):
                                    e.wait_ge(xh_done, CT * b + CT)
                                    e.wait_ge(xl_done, CT * b + CT)
                                col = {"qk": 0, "k0": 0, "k1": PART, "q0": C, "q1": C + PART}[u]
                                mm = project_in(e, slot, col, PART if L1 else 2 * K0)
                            elif u[0] == "v":
                                mm = project_values(e, slot, vcol + PART * int(u[1]))
                            elif u == "m":
                                q = i - first_m
                                tile = slice(q * PART, (q + 1) * PART)
                                if q == 0:
                                    if L1:
                                        e.wait_ge(hi_done, NQK * b + NQK)
                                    else:
                                        e.wait_ge(stack_dma, 16 * NSTACK * (b + 1))
                                for h in range(2):
                                    mv = slice(h * HALF, (h + 1) * HALF)
                                    terms = ([(QH[:, t, tile], KH[:, t, mv]) for t in range(CT)] if L1
                                             else [(QS[0:STACK, 0, 0, tile], KS[0:STACK, 0, 0, mv])])
                                    mm = split_products(e, psD[:, slot, mv], terms)
                            elif u == "T":
                                e.wait_ge(d_free, units_freed(b, i - 1))
                                mm = e.transpose(psD[0:NT, slot, 0:PART], MX[:, 0:NT], ident[:, :])
                            elif u[0] == "d":
                                h = int(u[1])
                                e.wait_ge(sum_done, (NT - 1) * (2 * b + h + 1))
                                mm = e.matmul(psD[:, slot, 0:HALF], ones[:, :], PA[:, 0:HALF], start=True, stop=True)
                            else:
                                e.wait_ge(out_done, 2 * b + 2)
                                mm = project_out(e, slot, int(u[1]))
                            mm.then_inc(d_full, 1)

                        def scores(s):
                            h, j = s // NT, s % NT
                            mv, tile = slice(h * HALF, (h + 1) * HALF), slice(j * PART, (j + 1) * PART)
                            if s >= 2:
                                e.wait_ge(exp_done, 2 * NT * b + s - 1)
                            if L1:
                                terms = [(kk[:, t, tile], qq[:, t, mv])
                                         for kk, qq in ((KH, QH), (KL, QH), (KH, QL)) for t in range(CT)]
                                terms.append((ONER[0:1, :], MR1[0:1, mv]))
                            else:
                                terms = [(KS[0:STACK + 1, 0, 0, tile], QS[0:STACK + 1, 0, 0, mv])]
                            split_products(e, psA[:, s % 2, :], terms).then_inc(st_full, 1)

                        def weigh(s):
                            h, j = s // NT, s % NT
                            if j == 0 and h == 1:
                                e.wait_ge(out_done, 2 * b + 1)
                            e.wait_ge(exp_done, 2 * NT * b + s + 1)
                            for t in range(CT):
                                mm = e.matmul(psO[:, t, :], V[:, t, j, :], PR[:, s % 8 // 2, (s % 2) * HALF:(s % 2) * HALF + HALF],
                                              start=(j == 0), stop=(j == NT - 1))
                            mm.then_inc(av_done, 1)

                        for i in range(at["T"] + 1):
                            unit(i)
                        e.wait_ge(row_dma, 16 * (b + 1))
                        if L1:
                            e.wait_ge(lo_done, NQK * b + NQK)
                        LAG = 2
                        for s in range(2 * NT + LAG):
                            if s < 2 * NT:
                                scores(s)
                            if s == NT + LAG:
                                unit(at["d0"])
                            if s >= LAG:
                                weigh(s - LAG)
                        for i in range(at["d1"], ND):
                            unit(i)

                @block.vector
                def _(e):
                    e.memset(TMP[:, :], 0.0).then_inc(d_free, 2)
                    with e.Fori(0, B) as b:
                        xb = X[:, bass.ds(b, 1)].rearrange("p b t n -> p (b t) n")
                        if L1:
                            norm_statistics(e, xb).then_inc(stat_done, 1)
                        for i, u in enumerate(units):
                            slot = i % 2
                            e.wait_ge(d_full, b * ND + i + 1)
                            full = psD[:, slot, :]
                            if u == "s":
                                e.tensor_copy(MV[:, :, :].rearrange("p a b -> p (a b)"), psD[:, slot, 0:4]).then_inc(d_free, 1)
                                group_variance(e).then_inc(var_done, 1)
                                e.wait_ge(rstd_done, b + 1)
                                norm_factors(e, 0, "gw1", "gb1")
                                for t in range(CT):
                                    e.tensor_scalar(SL[:, t, :], xb[:, t, :], SC[:, 0, t, 0:1], SC[:, 0, t, 1:2],
                                                    ALU.mult, ALU.add).then_inc(xn_done, 1)
                            elif u[0] in "kq":
                                q = i - (1 if L1 else 0)
                                if q >= 2:
                                    e.wait_ge(lo_done, NQK * b + q - 1)
                                p = PART if L1 else 2 * K0
                                e.tensor_scalar(SL[0:p, q % 2, :], full[0:p, :],
                                                par("bqk1", 4)[:, q:q + 1] if L1 else par("bqk0", 1, p),
                                                None, ALU.add).then_inc(d_free, 1)
                            elif u[0] == "v":
                                bias_values(e, slot, int(u[1])).then_inc(d_free, 1)
                            elif u == "m":
                                q = i - first_m
                                e.tensor_reduce(MX[:, q:q + 1], full, AX.X, ALU.max).then_inc(d_free, 1)
                            elif u == "T":
                                e.tensor_scalar(MROW[0:NT, :], psD[0:NT, slot, 0:PART], -1.0, None,
                                                ALU.mult).then_inc(d_free, 1)
                            elif u[0] == "d":
                                h = int(u[1])
                                mv = slice(h * HALF, (h + 1) * HALF)
                                e.reciprocal(RD[:, :], psD[:, slot, 0:HALF]).then_inc(d_free, 1)
                                e.drain()
                                e.wait_ge(av_done, 2 * NT * b + NT * (h + 1))
                                for t in range(CT):
                                    mul = e.tensor_tensor(A[:, t, mv], psO[:, t, :], RD[:, :], ALU.mult)
                                mul.then_inc(out_done, 1)
                                if not L1:
                                    e.drain()
                                    for t in range(CT):
                                        e.scalar_tensor_tensor(out=xb[:, t, mv], in0=A[:, t, mv], scalar=par("gamma0"),
                                                               in1=xb[:, t, mv], op0=ALU.mult, op1=ALU.add)
                            else:
                                o = int(u[1])
                                e.scalar_tensor_tensor(out=xb[:, o, :], in0=full, scalar=par("bp1", 2)[:, o:o + 1],
                                                       in1=xb[:, o, :], op0=ALU.add, op1=ALU.add).then_inc(d_free, 1)
                        e.drain()

                @block.scalar
                def _(e):
                    with e.Fori(0, B) as b:
                        for t in range(CT):
                            if L1:
                                e.wait_ge(xn_done, CT * b + t + 1)
                                src = SL[:, t, :]
                            else:
                                e.wait_ge(d_free, b * ND + 2)
                                src = X[:, bass.ds(b, 1), t, :].rearrange("p b n -> p (b n)")
                            e.activation(XH[:, t, :], src, ACT.Copy).then_inc(xh_done, 1)
                        for q in range(NQK):
                            i = q + (1 if L1 else 0)
                            e.wait_ge(d_free, units_freed(b, i))
                            if L1:
                                dst = (KH, KH, QH, QH)[q][:, q % 2, :]
                                e.activation(dst, SL[:, q % 2, :], ACT.Copy).then_inc(hi_done, 1)
                            else:
                                e.activation(SH[0:2 * K0, 0, :].bitcast(F32R), SL[0:2 * K0, 0, :], ACT.Copy).then_inc(hi_done, 1)
                        for s in range(2 * NT):
                            h, j = s // NT, s % NT
                            if h == 1:
                                e.wait_ge(av_done, 2 * NT * b + j + 1)
                                e.wait_ge(sum_done, 2 * (NT - 1) * b + max(j, 1))
                            e.wait_ge(st_full, 2 * NT * b + s + 1)
                            e.activation(PR[:, s % 8 // 2, (s % 2) * HALF:(s % 2) * HALF + HALF], psA[:, s % 2, :],
                                         ACT.Exp, scale=scale).then_inc(exp_done, 1)

                @block.gpsimd
                def _(e):
                    with e.Fori(0, B) as b:
                        if L1:
                            e.wait_ge(var_done, b + 1)
                            e.tensor_tensor(RSTD[:, :], VAR[:, :], MH[:, :], ALU.pow).then_inc(rstd_done, 1)
                        for t in range(CT):
                            e.wait_ge(xh_done, CT * b + t + 1)
                            src = SL[:, t, :] if L1 else X[:, bass.ds(b, 1), t, :].rearrange("p b n -> p (b n)")
                            e.tensor_tensor(XL[:, t, :], src, XH[:, t, :].bitcast(F32), ALU.subtract).then_inc(xl_done, 1)
                        for q in range(NQK):
                            e.wait_ge(hi_done, NQK * b + q + 1)
                            if L1:
                                hi = (KH, KH, QH, QH)[q][:, q % 2, :]
                                lo = (KL, KL, QL, QL)[q][:, q % 2, :]
                                e.tensor_tensor(lo, SL[:, q % 2, :], hi.bitcast(F32), ALU.subtract).then_inc(lo_done, 1)
                            else:
                                e.tensor_tensor(SL[0:2 * K0, 0, :].bitcast(F32R), SL[0:2 * K0, 0, :],
                                                SH[0:2 * K0, 0, :], ALU.subtract).then_inc(lo_done, 1)
                        for h in range(2):
                            for j in range(1, NT):
                                s = h * NT + j
                                slots = [PR[:, x % 8 // 2, (x % 2) * HALF:(x % 2) * HALF + HALF] for x in (s - 1, s)]
                                e.wait_ge(exp_done, 2 * NT * b + s + 1)
                                if j == 1 and h == 1:
                                    e.wait_ge(d_full, b * ND + at["d0"] + 1)
                                if j > 1:
                                    e.wait_ge(sum_done, (NT - 1) * (2 * b + h) + j - 1)
                                e.tensor_tensor(PA[:, 0:HALF], slots[0] if j == 1 else PA[:, 0:HALF], slots[1],
                                                ALU.add).then_inc(sum_done, 1)

                @block.sync
                def _(e):
                    for b in range(B):
                        if not L1:
                            e.wait_ge(lo_done, b + 1)
                            for dst, src in stack_copies([0]):
                                e.dma_start(dst, src).then_inc(stack_dma, 16)
                        e.wait_ge(d_free, units_freed(b, at["T"]))
                        row = MR1[0:1, :] if L1 else QS[STACK:STACK + 1, 0, 0, :]
                        e.dma_start(row.bitcast(F32), MROW[0:NT, :].bitcast(F32)).then_inc(row_dma, 16)
                        e.wait_ge(row_dma, 16 * (b + 1))

        def stack_copies(_):
            k, q = slice(0, K0), slice(K0, 2 * K0)
            for r, part in ((0, SH), (1, SL), (2, SH)):
                yield KS[r * K0:(r + 1) * K0, 0, 0, :].bitcast(F32), part[k, 0, :]
            for r, part in ((0, SH), (1, SH), (2, SL)):
                yield QS[r * K0:(r + 1) * K0, 0, 0, :].bitcast(F32), part[q, 0, :]

        def batch_norm():
            s_var, s_rstd, s_done = sem("bn_variance"), sem("bn_rstd"), sem("bn_done")
            with nc.Block() as block:
                @block.vector
                def _(e):
                    for t in range(CT):
                        for b in range(B):
                            for h in range(2):
                                e.bn_stats(BNS[:, t, 2 * b + h, :], X[:, b, t, h * HALF:(h + 1) * HALF])
                    e.drain()
                    for t in range(CT):
                        e.bn_aggr(MV[:, t, :], BNS[:, t].rearrange("p a b -> p (a b)"))
                    e.drain()
                    e.tensor_scalar(VAR[:, :], MV[:, :, 1], EPS, None, ALU.add).then_inc(s_var, 1)
                    e.wait_ge(s_rstd, 1)
                    norm_factors(e, 0, "bnw", "bnb")
                    for b in range(B):
                        for t in range(CT):
                            e.tensor_scalar(X[:, b, t, :], X[:, b, t, :], SC[:, 0, t, 0:1], SC[:, 0, t, 1:2],
                                            ALU.mult, ALU.add).then_inc(s_done, 1)
                    e.wait_ge(s_done, B * CT)

                @block.gpsimd
                def _(e):
                    e.wait_ge(s_var, 1)
                    e.tensor_tensor(RSTD[:, :], VAR[:, :], MH[:, :], ALU.pow).then_inc(s_rstd, 1)

        NGRP = B * GROUPS
        TAIL = 76 * B

        def side_units(g, first):
            if g == 0:
                pre = (["s0", "s1"] if first else []) + ["k", "q", "v"]
            else:
                pre = ["k", "q", "v", "s0", "s1"] + ([] if first else ["p0", "p1"])
            return pre + ["m"] * (QUADH * NT) + ["T"]

        def unit_base(G):
            if isinstance(G, int):
                return 0 if G == 0 else 38 if G == 1 else 76 * (G // 2) + 36 * (G % 2)
            raise ValueError

        def unit_steps(units):
            pre = len(units) - QUADH * NT - 1
            m0, m1 = 14, 57
            early = [0, 1, 2, 4, 5, 10, 11]
            return [early[i] if i < pre else m0 + (i - pre) * (m1 - m0) // (QUADH * NT) if i < len(units) - 1 else 58
                    for i in range(len(units))]

        QUAD_AT = [12, 13, 15, 19, 23, 27, 31, 35]

        def eight_heads(layer):
            load_weights(layer, 3 * C)
            scale = CH ** -0.5
            n = f"_{layer}"
            d_full, d_free = sem("unit_full" + n), sem("unit_free" + n)
            st_full, exp_done = sem("scores_full" + n), sem("exp_done" + n)
            av_done, sum_done, out_done = sem("av_done" + n), sem("sum_done" + n), sem("out_done" + n)
            stat_done, var_done, rstd_done = sem("stat_done" + n), sem("var_done" + n), sem("rstd_done" + n)
            xn_done, xh_done, xl_done = sem("xn_done" + n), sem("xh_done" + n), sem("xl_done" + n)
            hi_done, lo_done = sem("qk_high" + n), sem("qk_low" + n)
            stack_dma, row_dma = sem("stack_filled" + n), sem("max_row_filled" + n)
            s_out = sem("stored" + n)

            def wait(e, s, value):
                if not isinstance(value, int) or value > 0:
                    e.wait_ge(s, value)

            with nc.Block() as block:
                @block.tensor
                def _(e):
                    def weigh(P, p, J):
                        h, j = J // NT, J % NT
                        if j == 0:
                            wait(e, out_done, 2 * P + h)
                        wait(e, exp_done, STEPS * P + QUADH * (J + 1))
                        pr = PR[:, J % 4, :].rearrange("p (q n) -> p q n", q=QUADH)
                        for q in range(QUADH):
                            mm = e.matmul(psO[CH * q:CH * q + CH, 0, :], V[:, p, j, CH * q:CH * q + CH], pr[:, q, :],
                                          start=(j == 0), stop=(j == NT - 1))
                        sums = [pr] if j >= NT - DIRECT else []
                        if j == NT - 1:
                            wait(e, sum_done, ADDS * (2 * P + h + 1))
                            sums.append(PA[:, :].rearrange("p (q n) -> p q n", q=QUADH))
                        for k, ss in enumerate(sums):
                            for q in range(QUADH):
                                mm = e.matmul(psO[CH * q:CH * q + CH, 1, :], ones[:, 0:CH], ss[:, q, :],
                                              start=(j == NT - DIRECT), stop=(j == NT - 1 and k == 1))
                        mm.then_inc(av_done, 1)

                    def unit(u, k, i, G, g, t):
                        slot = i[1] % 2
                        wait(e, d_free, k - 1)
                        if u[0] == "s":
                            c = int(u[1])
                            wait(e, stat_done, t + 1)
                            mm = e.matmul(psD[:, slot, 0:2], gmat[:, :], GST[:, c, :], start=True, stop=True)
                        elif u in "kq":
                            if u == "k":
                                wait(e, xh_done, G + 2 - g)
                                wait(e, xl_done, G + 2 - g)
                            mm = project_in(e, slot, 2 * PART * g + (PART if u == "q" else 0), PART)
                        elif u == "v":
                            mm = project_values(e, slot, 2 * C + PART * g)
                        elif u == "m":
                            q, tile = i[0] // NT, i[0] % NT
                            if i[0] == 0:
                                wait(e, stack_dma, (G + 1) * 16 * DMAS)
                            for h in range(2):
                                mm = e.matmul(psD[:, slot, h * HALF:(h + 1) * HALF],
                                              QS[0:STACK, g, q, tile * PART:(tile + 1) * PART],
                                              KS[0:STACK, g, q, h * HALF:(h + 1) * HALF], start=True, stop=True)
                        elif u == "T":
                            wait(e, d_free, k)
                            mm = e.transpose(psD[0:QUADH * NT, slot, 0:PART], MX[:, :], ident[:, :])
                        else:
                            wait(e, out_done, t)
                            mm = project_out(e, slot, int(u[1]))
                        mm.then_inc(d_full, 1)

                    def phase(P, p, G, g, base, first, norm=None):
                        units = [] if G is None else side_units(g, first)
                        steps = unit_steps(units) if units else []
                        todo = list(enumerate(units))

                        def next_unit():
                            i, u = todo.pop(0)
                            m = i - (len(units) - QUADH * NT - 1)
                            t = norm if u[0] == "s" else P * 2 if u[0] == "p" else None
                            unit(u, base + i, (m, i), G, g, t)

                        if P is None:
                            while todo:
                                next_unit()
                            return
                        wait(e, row_dma, (P + 1) * 16 * QUADH)
                        for s in range(STEPS):
                            h, j, q = s // (NT * QUADH), s // QUADH % NT, s % QUADH
                            wait(e, exp_done, STEPS * P + s - 1)
                            e.matmul(psA[:, s % 2, :], KS[0:STACK + 1, p, q, j * PART:(j + 1) * PART],
                                     QS[0:STACK + 1, p, q, h * HALF:(h + 1) * HALF],
                                     start=True, stop=True).then_inc(st_full, 1)
                            while todo and steps[todo[0][0]] <= s:
                                next_unit()
                            if s == QUAD_AT[-1] - STEPS // 2 and not (isinstance(P, int) and P == 0):
                                weigh(P - 1, 1 - p, 2 * NT - 1)
                            for J in range(2 * NT):
                                if s == QUAD_AT[J % NT] + STEPS // 2 * (J // NT):
                                    weigh(P, p, J)

                    def tail():
                        weigh(NGRP - 1, 1, 2 * NT - 1)
                        for c in range(CT):
                            unit(f"p{c}", TAIL + c, (0, c), None, None, 2 * NGRP)

                    phase(None, None, 0, 0, 0, True, norm=0)
                    phase(0, 0, 1, 1, 38, True, norm=1)
                    with e.Fori(0, B - 1) as r:
                        phase(r * 2 + 1, 1, r * 2 + 2, 0, r * 76 + 76, False)
                        phase(r * 2 + 2, 0, r * 2 + 3, 1, r * 76 + 112, False, norm=r + 2)
                    phase(NGRP - 1, 1, None, None, TAIL, False)
                    tail()

                @block.vector
                def _(e):
                    def take_half(P, p, h):
                        wait(e, av_done, (2 * P + h + 1) * NT)
                        e.reciprocal(RD[:, :], psO[:, 1, :])
                        e.drain()
                        e.tensor_tensor(A[:, p, h * HALF:(h + 1) * HALF], psO[:, 0, :], RD[:, :],
                                        ALU.mult).then_inc(out_done, 1)

                    def batch(b):
                        return X[:, b] if isinstance(b, int) else X[:, bass.ds(b, 1)].rearrange("p b t n -> p (b t) n")

                    def factors(b):
                        return SC[:, b] if isinstance(b, int) else SC[:, bass.ds(b, 1)].rearrange("p b t n -> p (b t) n")

                    def add_residual(c, b, full):
                        xb, sc = batch(b), factors(b)
                        if layer == 2:
                            e.tensor_scalar(xb[:, c, :], xb[:, c, :], sc[:, c, 0:1], sc[:, c, 1:2], ALU.mult, ALU.add)
                            e.drain()
                        return e.scalar_tensor_tensor(out=xb[:, c, :], in0=full, scalar=par(f"bp{layer}", 2)[:, c:c + 1],
                                                      in1=xb[:, c, :], op0=ALU.add, op1=ALU.add)

                    def phase(P, p, G, g, base, first, proj=None, norm=None, norm_b=None):
                        units = [] if G is None else side_units(g, first)
                        steps = unit_steps(units) if units else []
                        events = [(steps[i], 0, "unit", i) for i in range(len(units))]
                        if norm is not None:
                            events.append((steps[units.index("s0")] - 0.5, 0, "stats", 0))
                            events.append((steps[units.index("s1")] + 0.2 if P is None else 22, 1, "xn", 0))
                        if P is not None:
                            if not (isinstance(P, int) and P == 0):
                                events.append((QUAD_AT[-1] - STEPS // 2 + 0.5, 0, "half", -1))
                            events.append((QUAD_AT[-1] + 0.5, 0, "half", 0))
                        for _, _, what, i in sorted(events):
                            if what == "half":
                                take_half(P - 1 if i < 0 else P, 1 - p if i < 0 else p, 1 if i < 0 else 0)
                                continue
                            if what == "stats":
                                norm_statistics(e, batch(norm_b)).then_inc(stat_done, 1)
                                continue
                            if what == "xn":
                                e.wait_ge(rstd_done, norm + 1)
                                norm_factors_at(norm_b)
                                if P is not None:
                                    wait(e, stack_dma, (G + 1) * 16 * DMAS)
                                xb, sc = batch(norm_b), factors(norm_b)
                                for c in range(CT):
                                    e.tensor_scalar(SL[:, c, :], xb[:, c, :], sc[:, c, 0:1], sc[:, c, 1:2],
                                                    ALU.mult, ALU.add).then_inc(xn_done, 1)
                                continue
                            u, slot = units[i], i % 2
                            e.wait_ge(d_full, base + i + 1)
                            full = psD[:, slot, :]
                            if u[0] == "s":
                                e.tensor_copy(MV[:, int(u[1]), :], psD[:, slot, 0:2]).then_inc(d_free, 1)
                                if u == "s1":
                                    group_variance(e).then_inc(var_done, 1)
                            elif u in "kq":
                                w = "kq".index(u)
                                wait(e, stack_dma, G * 16 * DMAS)
                                if isinstance(G, int) and G == 0:
                                    e.wait_ge(xl_done, CT)
                                e.tensor_scalar(SL[:, w, :], full, par(f"bqk{layer}", 4)[:, 2 * g + w:2 * g + w + 1], None,
                                                ALU.add).then_inc(d_free, 1)
                            elif u == "v":
                                wait(e, av_done, (G - 1) * 2 * NT)
                                bias_values(e, slot, g).then_inc(d_free, 1)
                            elif u == "m":
                                m = i - (len(units) - QUADH * NT - 1)
                                e.tensor_reduce(MX[:, m:m + 1], full, AX.X, ALU.max).then_inc(d_free, 1)
                            elif u == "T":
                                wait(e, row_dma, G * 16 * QUADH)
                                e.tensor_scalar(MROW[:, :], psD[0:QUADH * NT, slot, 0:PART], -1.0, None,
                                                ALU.mult).then_inc(d_free, 1)
                            else:
                                add_residual(int(u[1]), proj, full).then_inc(d_free, 1)

                    def norm_factors_at(b):
                        sc = factors(b)
                        e.tensor_tensor(sc[:, :, 0], RSTD[:, :], par(f"gw{layer}", 2), ALU.mult)
                        e.drain()
                        e.tensor_tensor(TMP[:, :], MV[:, :, 0], sc[:, :, 0], ALU.mult)
                        e.drain()
                        e.tensor_tensor(sc[:, :, 1], par(f"gb{layer}", 2), TMP[:, :], ALU.subtract)
                        e.drain()

                    phase(None, None, 0, 0, 0, True, norm=0, norm_b=0)
                    phase(0, 0, 1, 1, 38, True, norm=1, norm_b=1)
                    with e.Fori(0, B - 1) as r:
                        phase(r * 2 + 1, 1, r * 2 + 2, 0, r * 76 + 76, False)
                        phase(r * 2 + 2, 0, r * 2 + 3, 1, r * 76 + 112, False, proj=r, norm=r + 2, norm_b=(r + 2) % B)
                    phase(NGRP - 1, 1, None, None, TAIL, False)
                    take_half(NGRP - 1, 1, 1)
                    for c in range(CT):
                        e.wait_ge(d_full, TAIL + c + 1)
                        add_residual(c, B - 1, psD[:, c % 2, :]).then_inc(d_free, 1)
                    e.drain()

                @block.scalar
                def _(e):
                    def phase(P, p, G, g, base, first, norm=None):
                        units = [] if G is None else side_units(g, first)
                        steps = unit_steps(units) if units else []
                        events = []
                        if units:
                            for w in range(2):
                                i = units.index("kq"[w])
                                events.append((steps[i] + 3 + w, "high", (w, base + i)))
                        if norm is not None:
                            events += [(-1 if P is None else 28 + 3 * c, "xh", c) for c in range(CT)]
                        events.sort()

                        def run(what, a):
                            if what == "high":
                                w, k = a
                                e.wait_ge(d_free, k + 1)
                                wait(e, stack_dma, G * 16 * DMAS)
                                e.activation(SH[:, w, :].bitcast(F32R), SL[:, w, :], ACT.Copy).then_inc(hi_done, 1)
                            else:
                                e.wait_ge(xn_done, CT * norm + a + 1)
                                if P is not None:
                                    e.wait_ge(d_free, base + units.index("v") + 1)
                                e.activation(XH[:, a, :], SL[:, a, :], ACT.Copy).then_inc(xh_done, 1)

                        if P is None:
                            for _, what, a in events:
                                run(what, a)
                            return
                        for s in range(STEPS):
                            J = s // QUADH
                            if s % QUADH == 0:
                                if J >= 4:
                                    wait(e, av_done, 2 * NT * P + J - 3)
                                    h, j = (J - 4) // NT, (J - 4) % NT
                                    wait(e, sum_done, ADDS * (2 * P + h) + min(max(j, 1), ADDS))
                                else:
                                    wait(e, av_done, 2 * NT * P + J - 3)
                                    wait(e, sum_done, ADDS * 2 * P)
                            wait(e, st_full, STEPS * P + s + 1)
                            e.activation(PR[:, J % 4, (s % QUADH) * HALF:(s % QUADH + 1) * HALF], psA[:, s % 2, :],
                                         ACT.Exp, scale=scale).then_inc(exp_done, 1)
                            while events and events[0][0] <= s:
                                run(*events.pop(0)[1:])

                    phase(None, None, 0, 0, 0, True, norm=0)
                    phase(0, 0, 1, 1, 38, True, norm=1)
                    with e.Fori(0, B - 1) as r:
                        phase(r * 2 + 1, 1, r * 2 + 2, 0, r * 76 + 76, False)
                        phase(r * 2 + 2, 0, r * 2 + 3, 1, r * 76 + 112, False, norm=r + 2)
                    phase(NGRP - 1, 1, None, None, TAIL, False)

                @block.gpsimd
                def _(e):
                    def rstd(norm):
                        e.wait_ge(var_done, norm + 1)
                        e.tensor_tensor(RSTD[:, :], VAR[:, :], MH[:, :], ALU.pow).then_inc(rstd_done, 1)

                    def input_low(norm):
                        for c in range(CT):
                            e.wait_ge(xh_done, CT * norm + c + 1)
                            e.tensor_tensor(XL[:, c, :], SL[:, c, :], XH[:, c, :].bitcast(F32),
                                            ALU.subtract).then_inc(xl_done, 1)

                    def stack_low(G):
                        for w in range(2):
                            e.wait_ge(hi_done, G * 2 + w + 1)
                            e.tensor_tensor(SL[:, w, :].bitcast(F32R), SL[:, w, :], SH[:, w, :],
                                            ALU.subtract).then_inc(lo_done, 1)

                    def phase(P, G, norm=None):
                        if P is None:
                            rstd(norm)
                            input_low(norm)
                            stack_low(G)
                            return
                        if G is not None:
                            stack_low(G)
                        for h in range(2):
                            for j in range(1, ADDS + 1):
                                J = h * NT + j
                                wait(e, exp_done, STEPS * P + QUADH * (J + 1))
                                if j == 1:
                                    wait(e, av_done, NT * (2 * P + h))
                                else:
                                    wait(e, sum_done, ADDS * (2 * P + h) + j - 1)
                                e.tensor_tensor(PA[:, :], PR[:, (J - 1) % 4, :] if j == 1 else PA[:, :],
                                                PR[:, J % 4, :], ALU.add).then_inc(sum_done, 1)
                                if norm is not None and h == 0 and j == 1:
                                    rstd(norm)
                            if norm is not None and h == 0:
                                input_low(norm)

                    phase(None, 0, norm=0)
                    phase(0, 1, norm=1)
                    with e.Fori(0, B - 1) as r:
                        phase(r * 2 + 1, r * 2 + 2)
                        phase(r * 2 + 2, r * 2 + 3, norm=r + 2)
                    phase(NGRP - 1, None)

                @block.sync
                def _(e):
                    for G in range(NGRP):
                        g = G % 2
                        e.wait_ge(lo_done, 2 * G + 2)
                        wait(e, st_full, STEPS * (G - 1))
                        for q in range(QUADH):
                            rows = slice(CH * q, CH * (q + 1))
                            for r in range(3):
                                dst = slice(CH * r, CH * (r + 1))
                                e.dma_start(KS[dst, g, q, :].bitcast(F32), (SH, SL, SH)[r][rows, 0, :]).then_inc(stack_dma, 16)
                                e.dma_start(QS[dst, g, q, :].bitcast(F32), (SH, SH, SL)[r][rows, 1, :]).then_inc(stack_dma, 16)
                        e.wait_ge(d_free, unit_base(G) + len(side_units(g, G < 2)))
                        for q in range(QUADH):
                            e.dma_start(QS[STACK:STACK + 1, g, q, :].bitcast(F32),
                                        MROW[NT * q:NT * (q + 1), :].bitcast(F32)).then_inc(row_dma, 16)
                        if layer == 3 and g == 1 and G > 1:
                            b = G // 2 - 1
                            e.dma_start(out_v[:, b], X[:, b]).then_inc(s_out, 16)
                    if layer == 3:
                        e.wait_ge(d_free, TAIL + CT)
                        e.dma_start(out_v[:, B - 1], X[:, B - 1]).then_inc(s_out, 16)
                        e.wait_ge(s_out, 16 * B)

        single_head(0)
        batch_norm()
        single_head(1)
        eight_heads(2)
        eight_heads(3)


def laid_out(inputs):
    import numpy as np

    f = {k: np.asarray(v) for k, v in inputs.items()}
    ident = np.eye(PART, dtype=np.float32)
    gmat = np.kron(np.eye(PART // 8), np.full((8, 8), 1 / 8)).astype(np.float32)
    par = np.zeros((PART, NPAR), np.float32)

    def put(name, v):
        v = np.asarray(v).reshape(-1)
        for i in range(max(1, len(v) // PART)):
            w = v[i * PART:(i + 1) * PART]
            par[:len(w), PC[name] + i] = w

    par[:, PC["gamma0"]] = f["L0_conv_gamma"]
    put("bnw", f["L0_conv_bn_w"])
    put("bnb", f["L0_conv_bn_b"])
    put("bqk0", np.concatenate([f["L0_conv_bk"], f["L0_conv_bq"]]))
    w, bv, wp = [], [], []
    w.append(np.concatenate([f["L0_conv_Wk"], f["L0_conv_Wq"], f["L0_conv_Wv"]]))
    bv.append(f["L0_conv_bv"])
    order = np.concatenate([np.arange(C, 2 * C), np.arange(C), np.arange(2 * C, 3 * C)])
    orders = {1: order}
    rows = np.arange(3 * C).reshape(HEADS, 3, CH)
    parts = [rows[g * QUADH:(g + 1) * QUADH, k].reshape(-1) for g in range(GROUPS) for k in (1, 0)]
    orders[2] = orders[3] = np.concatenate(parts + [rows[:, 2].reshape(-1)])
    norm = {1: ("gamma", "beta"), 2: ("gn_w", "gn_b"), 3: ("norm_scale", "norm_bias")}
    for n in (1, 2, 3):
        pre = f"L{n}_conv_"
        wl, bl = f[pre + "qkv_w"][orders[n]], f[pre + "qkv_b"][orders[n]]
        w.append(wl)
        bv.append(bl[2 * C:])
        wp.append(f[pre + "proj_w"])
        put(f"gw{n}", f[pre + norm[n][0]])
        put(f"gb{n}", f[pre + norm[n][1]])
        put(f"bp{n}", f[pre + "proj_b"])
        put(f"bqk{n}", bl[:2 * C])
    arrays = {"x": np.ascontiguousarray(f["x"].reshape(B, C, N))}
    for n in range(4):
        arrays[f"w{n}"] = np.ascontiguousarray(w[n].T)
    for n in (1, 2, 3):
        arrays[f"wp{n}"] = np.ascontiguousarray(wp[n - 1].T)
    for n in range(4):
        arrays[f"bv{n}"] = np.ascontiguousarray(np.broadcast_to(bv[n], (PART, C)))
    arrays |= {"par": par, "ident": ident, "gmat": gmat}
    return arrays


def kernel(**inputs):
    import concourse.bacc as bacc
    from concourse.bass_utils import run_bass_kernel_spmd

    nc = bacc.Bacc("TRN2", target_bir_lowering=False, num_devices=1)
    arrays = laid_out(inputs)
    args = [nc.dram_tensor(k, a.shape, mybir.dt.from_np(a.dtype), kind="ExternalInput").ap() for k, a in arrays.items()]
    args.append(nc.dram_tensor("out", (B, C, N), F32, kind="ExternalOutput").ap())
    attention_stack(nc, *args)
    r = run_bass_kernel_spmd(nc, [arrays], core_ids=[0])
    return r.results[0]["out"].reshape(B, C, 32, 32)
```

```python
from contextlib import ExitStack

import concourse.bass as bass
from concourse import mybir

ALU = mybir.AluOpType
ACT = mybir.ActivationFunctionType
AX = mybir.AxisListType
F32 = mybir.dt.float32
F32R = mybir.dt.float32r
BF16 = mybir.dt.bfloat16

B, C, N = 4, 256, 1024
PART = 128
CT = C // PART
NT = N // PART
HALF = N // 2
HEADS, CH = 8, 32
QUADH = 4
GROUPS = HEADS // QUADH
K0 = C // 8
STACK = 3 * CH
EPS = 1e-5

STEPS = 2 * NT * QUADH
DIRECT = 3
ADDS = NT - DIRECT - 1
STACK_DMAS = 6

PC = {"gamma0": 0, "bnw": 1, "bnb": 3, "bqk0": 5}
for _n, _l in enumerate((1, 2, 3)):
    for _k, _f in enumerate(("gw", "gb", "bp", "bv", "bqk")):
        PC[f"{_f}{_l}"] = 6 + 12 * _n + 2 * _k
NPAR = 6 + 12 * 3


def attention_stack(nc, x, w0, w1, w2, w3, wp1, wp2, wp3, bv0, bv1, par_d, ident_d, gmat_d, out):
    with ExitStack() as ctx:
        def sb(name, shape, dt=F32):
            return ctx.enter_context(nc.sbuf_tensor(name, shape, dt))

        def sem(name):
            return ctx.enter_context(nc.semaphore(name))

        X = sb("X", [PART, B, CT, N])
        XH = sb("XH", [PART, CT, N], F32R)
        XL = sb("XL", [PART, CT, N], F32R)
        SH = sb("SH", [PART, 2, N])
        SL = sb("SL", [PART, 2, N])
        KS = sb("KS", [PART, 2, QUADH, N], F32R)
        QS = sb("QS", [PART, 2, QUADH, N], F32R)
        V = sb("V", [PART, GROUPS, NT, PART])
        PR = sb("PR", [PART, 4, QUADH * HALF])
        PA = sb("PA", [PART, QUADH * HALF])
        A = sb("A", [PART, CT, N])
        WH = sb("WH", [PART, CT, 3 * C], F32R)
        WL = sb("WL", [PART, CT, 3 * C], F32R)
        WP = sb("WP", [PART, CT, C])
        VT = sb("VT", [PART, N])
        BV = VT[:, 0:C]
        PAR = sb("PAR", [PART, NPAR])
        ident = sb("identity", [PART, PART])
        gmat = sb("group_mean", [PART, PART])
        ones = sb("ones", [PART, PART])
        MX = sb("MX", [PART, 32])
        MROW = sb("MROW", [32, PART], F32R)
        BST = sb("BST", [PART, CT, 2, 6])
        MV = sb("MV", [PART, CT, 2])
        GST = sb("GST", [PART, CT, 2])
        VAR = sb("VAR", [PART, CT])
        RSTD = sb("RSTD", [PART, CT])
        MH = sb("MH", [PART, CT])
        SC = sb("SC", [PART, B, CT, 2])
        BNS = sb("BNS", [PART, CT, B * 2, 6])
        MXH = BNS[:, :, :, :].rearrange("p a b c -> p (a b c)")[:, 0:2 * 32].rearrange("p (h q t) -> p h q t", h=2, q=QUADH)
        TMP = sb("TMP", [PART, CT])
        ONEB = sb("ONEB", [2, PART], BF16)
        MRB = sb("MRB", [NT, 2, PART], BF16)
        MR1 = sb("MR1", [2, N], BF16)

        psD = ctx.enter_context(nc.psum_tensor("psD", [PART, 2, N], F32))
        psA = ctx.enter_context(nc.psum_tensor("psA", [PART, 2, HALF], F32))
        psO = ctx.enter_context(nc.psum_tensor("psO", [PART, 2, HALF], F32))

        def par(name, n=1, p=PART):
            return PAR[0:p, PC[name]:PC[name] + n]


        x_v = x.rearrange("b (t p) n -> p b t n", p=PART)
        out_v = out.rearrange("b (t p) n -> p b t n", p=PART)
        w_dram = [w.rearrange("(t p) n -> p t n", p=PART) for w in (w0, w1, w2, w3)]
        wp_dram = [None] + [w.rearrange("(t p) n -> p t n", p=PART) for w in (wp1, wp2, wp3)]
        bv_dram = [bv0, bv1]

        s_x, s_const, s_memset = sem("x_loaded"), sem("constants_loaded"), sem("memsets_done")
        with nc.Block() as block:
            @block.sync
            def _(e):
                for tile, d in ((PAR, par_d), (ident, ident_d), (gmat, gmat_d)):
                    e.dma_start(tile[:, :], d).then_inc(s_const, 16)
                for b in range(B):
                    e.dma_start(X[:, b], x_v[:, b]).then_inc(s_x, 16)

            @block.vector
            def _(e):
                e.memset(ones[:, :], 1.0).then_inc(s_memset, 1)
                e.memset(MH[:, :], -0.5).then_inc(s_memset, 1)
                e.memset(KS[STACK:STACK + 1].bitcast(F32), 1.0).then_inc(s_memset, 1)
                e.memset(ONEB[:, :], 1.0).then_inc(s_memset, 1)
                e.wait_ge(s_memset, 4)
                e.wait_ge(s_x, 16 * B)
                e.wait_ge(s_const, 48)

        def load_weights(layer, wide):
            s_w, s_wh, s_wl = sem(f"w_loaded{layer}"), sem(f"w_high{layer}"), sem(f"w_low{layer}")
            n = 3 if layer == 1 else 2
            raw = SL[:, :, :].rearrange("p t n -> p (t n)")[:, 0:CT * wide].rearrange("p (t n) -> p t n", t=CT)
            with nc.Block() as block:
                @block.sync
                def _(e):
                    e.dma_start(raw, w_dram[layer]).then_inc(s_w, 16)
                    if layer < 2:
                        e.dma_start(BV, bv_dram[layer]).then_inc(s_w, 16)
                    if layer:
                        e.dma_start(WP[:, :, :], wp_dram[layer]).then_inc(s_w, 16)

                @block.vector
                def _(e):
                    if layer == 2:
                        e.memset(KS[STACK:STACK + 1].bitcast(F32), 1.0)
                    e.wait_ge(s_w, 16 * n)
                    e.tensor_copy(WH[:, :, 0:wide], raw).then_inc(s_wh, 1)
                    e.wait_ge(s_wh, 1)
                    e.tensor_tensor(WL[:, :, 0:wide], raw, WH[:, :, 0:wide], ALU.subtract).then_inc(s_wl, 1)
                    e.wait_ge(s_wl, 1)

        def split_products(e, out_ap, terms):
            last = None
            for i, (w, m) in enumerate(terms):
                last = e.matmul(out_ap, w, m, start=(i == 0), stop=(i == len(terms) - 1))
            return last

        def project_in(e, slot, col, width, halves=(0, 1)):
            for h in halves:
                mv = slice(h * HALF, (h + 1) * HALF)
                terms = [(w[:, t, col:col + width], xx[:, t, mv])
                         for w, xx in ((WH, XH), (WL, XH), (WH, XL)) for t in range(CT)]
                last = split_products(e, psD[0:width, slot, mv], terms)
            return last

        def project_values(e, slot, col, i):
            for n in range(NT // 2):
                st = slice((NT // 2 * i + n) * PART, (NT // 2 * i + n + 1) * PART)
                terms = [(xx[:, t, st], w[:, t, col:col + C])
                         for xx, w in ((XH, WH), (XL, WH), (XH, WL)) for t in range(CT)]
                last = split_products(e, psD[:, slot, n * C:(n + 1) * C], terms)
            return last

        def project_out(e, slot, o, halves=(0, 1)):
            for h in halves:
                mv = slice(h * HALF, (h + 1) * HALF)
                last = split_products(e, psD[:, slot, mv],
                                      [(WP[:, t, o * PART:(o + 1) * PART], A[:, t, mv]) for t in range(CT)])
            return last

        def values_of(slot):
            return V[:, :, :, :] if slot == 0 else PR[:, 2, :].rearrange("p (g t c) -> p g t c", g=CT, t=NT)

        def bias_values(e, slot, vslot, i):
            out_ap = values_of(vslot).rearrange("p g t c -> p t g c")[:, NT // 2 * i:NT // 2 * (i + 1)]
            full = psD[:, slot, :].rearrange("p (t g c) -> p t g c", t=NT // 2, g=CT)
            bias = BV.rearrange("p (g c) -> p g c", g=CT).unsqueeze(1).broadcast_to((PART, NT // 2, CT, PART))
            return e.tensor_tensor(out_ap, full, bias, ALU.add)

        def norm_statistics(e, xb):
            for t in range(CT):
                for h in range(2):
                    e.bn_stats(BST[:, t, h, :], xb[:, t, h * HALF:(h + 1) * HALF])
            e.drain()
            for t in range(CT):
                e.bn_aggr(MV[:, t, :], BST[:, t, :, :].rearrange("p a b -> p (a b)"))
            e.drain()
            e.tensor_tensor(GST[:, :, 1], MV[:, :, 0], MV[:, :, 0], ALU.mult)
            e.drain()
            e.tensor_tensor(GST[:, :, 1], GST[:, :, 1], MV[:, :, 1], ALU.add)
            return e.tensor_copy(GST[:, :, 0], MV[:, :, 0])

        def group_variance(e):
            e.drain()
            e.tensor_tensor(TMP[:, :], MV[:, :, 0], MV[:, :, 0], ALU.mult)
            e.drain()
            e.tensor_tensor(TMP[:, :], MV[:, :, 1], TMP[:, :], ALU.subtract)
            e.drain()
            return e.tensor_scalar(VAR[:, :], TMP[:, :], EPS, None, ALU.add)

        def norm_factors(e, b, gw, gb):
            e.tensor_tensor(SC[:, b, :, 0], RSTD[:, :], par(gw, 2), ALU.mult)
            e.drain()
            e.tensor_tensor(TMP[:, :], MV[:, :, 0], SC[:, b, :, 0], ALU.mult)
            e.drain()
            e.tensor_tensor(SC[:, b, :, 1], par(gb, 2), TMP[:, :], ALU.subtract)
            e.drain()

        def wait(e, s, value):
            if not isinstance(value, int) or value > 0:
                e.wait_ge(s, value)

        WEIGH_AT = [4, 4, 5, 5, 6, 7, 8, 9]

        def single_head(layer):
            wide = (2 * K0 if layer == 0 else 2 * C) + C
            load_weights(layer, wide)
            L1 = layer == 1
            vcol = wide - C
            scale = 1.0 if layer == 0 else C ** -0.5
            NQK = 4 if L1 else 1
            NSTACK = 6
            NROW = 2 if L1 else 1
            S = 2 * NT
            n = f"_{layer}"
            d_full, d_free = sem("unit_full" + n), sem("unit_free" + n)
            st_full, exp_done = sem("scores_full" + n), sem("exp_done" + n)
            av_done, sum_done, out_done = sem("av_done" + n), sem("sum_done" + n), sem("out_done" + n)
            stat_done, var_done, rstd_done = sem("stat_done" + n), sem("var_done" + n), sem("rstd_done" + n)
            xn_done, xh_done, xl_done = sem("xn_done" + n), sem("xh_done" + n), sem("xl_done" + n)
            hi_done, lo_done = sem("qk_high" + n), sem("qk_low" + n)
            stack_dma, row_dma = sem("stack_filled" + n), sem("max_row_filled" + n)

            prep = ([("s", 0)] if L1 else []) + [("qk", i) for i in range(NQK)] + [("v", 0), ("v", 1)]
            prep += [("m", i) for i in range(NT)] + [("T", 0)]
            if L1:
                prep_at = [0, 5, 5, 6, 6, 7, 8, 11, 11, 12, 12, 13, 13, 14, 14, 15]
            else:
                prep_at = [3, 4, 5, 7, 8, 8, 9, 11, 11, 12, 12, 14]
            plan = {}
            index = {}
            for P in range(-1, B + 1):
                ev = []
                if P + 1 < B:
                    ev += [(at if P >= 0 else -1, k, u, i, P + 1) for k, ((u, i), at) in enumerate(zip(prep, prep_at))]
                if 0 <= P < B:
                    ev.append((10, -1, "sum", 0, P))
                if P > 0:
                    ev.append((2, -1, "sum", 1, P - 1))
                    if L1:
                        ev += [(4, -1, "p", c, P - 1) for c in range(CT)]
                plan[P] = [(at, u, i, b) for at, _, u, i, b in sorted(ev, key=lambda x: (x[0], x[1], x[3]))]
                for _, u, i, b in plan[P]:
                    index[u, i, b] = len(index)

            def keys(slot):
                return KS[:, slot, 0:2], KS[:, slot, 2:4]

            def queries(slot):
                return QS[:, slot, 0:2], QS[:, slot, 2:4]

            def pr_slot(s):
                return PR[:, s % 8 // 4, (s % 4) * HALF:(s % 4 + 1) * HALF]

            with nc.Block() as block:
                @block.tensor
                def _(e):
                    def unit(u, i, b):
                        k = index[u, i, b]
                        slot, buf = k % 2, b % 2
                        wait(e, d_free, k - 1)
                        if u == "s":
                            e.wait_ge(stat_done, b + 1)
                            mm = e.matmul(psD[:, slot, 0:4], gmat[:, :], GST[:, :, :].rearrange("p a b -> p (a b)"),
                                          start=True, stop=True)
                        elif u == "qk":
                            if i == 0:
                                e.wait_ge(xh_done, CT * (b + 1))
                                e.wait_ge(xl_done, CT * (b + 1))
                            mm = project_in(e, slot, PART * i, PART if L1 else 2 * K0)
                        elif u == "v":
                            mm = project_values(e, slot, vcol, i)
                        elif u == "m":
                            tile = slice(i * PART, (i + 1) * PART)
                            if i == 0:
                                if L1:
                                    e.wait_ge(hi_done, NQK * (b + 1))
                                else:
                                    e.wait_ge(stack_dma, 16 * NSTACK * (b + 1))
                            for h in range(2):
                                mv = slice(h * HALF, (h + 1) * HALF)
                                terms = ([(queries(buf)[0][:, t, tile], keys(buf)[0][:, t, mv]) for t in range(CT)] if L1
                                         else [(QS[0:STACK, buf, 0, tile], KS[0:STACK, buf, 0, mv])])
                                mm = split_products(e, psD[:, slot, mv], terms)
                        elif u == "T":
                            e.wait_ge(d_free, k)
                            mm = e.transpose(psD[0:NT, slot, 0:PART], MX[:, 0:NT], ident[:, :])
                        elif u == "sum":
                            e.wait_ge(sum_done, (NT - 1) * (2 * b + i + 1))
                            mm = e.matmul(psD[:, slot, 0:HALF], ones[:, :], PA[:, i * HALF:(i + 1) * HALF],
                                          start=True, stop=True)
                        else:
                            e.wait_ge(out_done, 2 * (b + 1))
                            mm = project_out(e, slot, i)
                        mm.then_inc(d_full, 1)

                    def scores(P, s):
                        h, j = s // NT, s % NT
                        mv, tile = slice(h * HALF, (h + 1) * HALF), slice(j * PART, (j + 1) * PART)
                        wait(e, exp_done, S * P + s - 1)
                        if L1:
                            (kh, kl), (qh, ql) = keys(P % 2), queries(P % 2)
                            for i, (kk, qq) in enumerate(((kh, qh), (kl, qh), (kh, ql))):
                                for t in range(CT):
                                    e.matmul(psA[:, s % 2, :], kk[:, t, tile], qq[:, t, mv], start=(i == t == 0), stop=False)
                            mm = e.matmul(psA[:, s % 2, :], ONEB[:, :], MR1[:, mv], start=False, stop=True)
                        else:
                            mm = e.matmul(psA[:, s % 2, :], KS[0:STACK + 1, P % 2, 0, tile],
                                          QS[0:STACK + 1, P % 2, 0, mv], start=True, stop=True)
                        mm.then_inc(st_full, 1)

                    def weigh(P, s):
                        h, j = s // NT, s % NT
                        if j == 0:
                            wait(e, out_done, 2 * P + h)
                        e.wait_ge(exp_done, S * P + s + 1)
                        for t in range(CT):
                            mm = e.matmul(psO[:, t, :], values_of(P % 2)[:, t, j, :], pr_slot(s),
                                          start=(j == 0), stop=(j == NT - 1))
                        mm.then_inc(av_done, 1)

                    for P in range(-1, B + 1):
                        todo = list(plan[P])
                        if 0 <= P < B:
                            e.wait_ge(row_dma, 16 * NROW * (P + 1))
                            if L1:
                                e.wait_ge(lo_done, NQK * (P + 1))
                            for s in range(S):
                                scores(P, s)
                                for x in range(S):
                                    if WEIGH_AT[x % NT] + NT * (x // NT) == s + S and P > 0:
                                        weigh(P - 1, x)
                                for x in range(S):
                                    if WEIGH_AT[x % NT] + NT * (x // NT) == s:
                                        weigh(P, x)
                                while todo and todo[0][0] <= s:
                                    unit(*todo.pop(0)[1:])
                        elif P == B:
                            weigh(B - 1, S - 2)
                            weigh(B - 1, S - 1)
                        for x in todo:
                            unit(*x[1:])

                @block.vector
                def _(e):
                    for P in range(-1, B + 1):
                        stats_left = L1 and P + 1 < B
                        if stats_left:
                            norm_statistics(e, X[:, P + 1]).then_inc(stat_done, 1)
                        for _, u, i, b in plan[P]:
                            k = index[u, i, b]
                            slot = k % 2
                            full = psD[:, slot, :]
                            e.wait_ge(d_full, k + 1)
                            if u == "s":
                                e.tensor_copy(MV[:, :, :].rearrange("p a b -> p (a b)"), psD[:, slot, 0:4]).then_inc(d_free, 1)
                                group_variance(e).then_inc(var_done, 1)
                                e.wait_ge(rstd_done, b + 1)
                                norm_factors(e, 0, "gw1", "gb1")
                                wait(e, lo_done, NQK * b)
                                for t in range(CT):
                                    e.tensor_scalar(SL[:, t, :], X[:, b, t, :], SC[:, 0, t, 0:1], SC[:, 0, t, 1:2],
                                                    ALU.mult, ALU.add).then_inc(xn_done, 1)
                            elif u == "qk":
                                if i >= 2:
                                    e.wait_ge(lo_done, NQK * b + i - 1)
                                if not L1:
                                    wait(e, stack_dma, 16 * NSTACK * b)
                                p = PART if L1 else 2 * K0
                                e.tensor_scalar(SL[0:p, i % 2, :], full[0:p, :],
                                                par("bqk1", 4)[:, i:i + 1] if L1 else par("bqk0", 1, p),
                                                None, ALU.add).then_inc(d_free, 1)
                            elif u == "v":
                                wait(e, av_done, S * (b - 1))
                                bias_values(e, slot, b % 2, i).then_inc(d_free, 1)
                            elif u == "m":
                                e.tensor_reduce(MX[:, i:i + 1], full, AX.X, ALU.max).then_inc(d_free, 1)
                            elif u == "T":
                                wait(e, row_dma, 16 * NROW * b)
                                top = psD[0:NT, slot, 0:PART]
                                if L1:
                                    e.tensor_scalar(MRB[:, 0, :], top, -1.0, None, ALU.mult)
                                    e.drain()
                                    e.scalar_tensor_tensor(out=MRB[:, 1, :], in0=top, scalar=-1.0, in1=MRB[:, 0, :],
                                                           op0=ALU.mult, op1=ALU.subtract).then_inc(d_free, 1)
                                else:
                                    e.tensor_scalar(MROW[0:NT, :], top, -1.0, None, ALU.mult).then_inc(d_free, 1)
                            elif u == "sum":
                                mv = slice(i * HALF, (i + 1) * HALF)
                                e.reciprocal(VT[:, HALF:N], psD[:, slot, 0:HALF]).then_inc(d_free, 1)
                                e.drain()
                                e.wait_ge(av_done, S * b + NT * (i + 1))
                                for t in range(CT):
                                    mul = e.tensor_tensor(A[:, t, mv], psO[:, t, :], VT[:, HALF:N], ALU.mult)
                                mul.then_inc(out_done, 1)
                                e.drain()
                                if not L1:
                                    for t in range(CT):
                                        e.scalar_tensor_tensor(out=X[:, b, t, mv], in0=A[:, t, mv], scalar=par("gamma0"),
                                                               in1=X[:, b, t, mv], op0=ALU.mult, op1=ALU.add)
                            else:
                                e.scalar_tensor_tensor(out=X[:, b, i, :], in0=full, scalar=par("bp1", 2)[:, i:i + 1],
                                                       in1=X[:, b, i, :], op0=ALU.add, op1=ALU.add).then_inc(d_free, 1)
                    e.drain()

                @block.scalar
                def _(e):
                    def high(b, t):
                        if L1:
                            e.wait_ge(xn_done, CT * b + t + 1)
                            src = SL[:, t, :]
                        else:
                            src = X[:, b, t, :]
                        if b:
                            e.wait_ge(d_full, index["v", 1, b - 1] + 1)
                        e.activation(XH[:, t, :], src, ACT.Copy).then_inc(xh_done, 1)

                    def qk_high(b, i):
                        e.wait_ge(d_free, index["qk", i, b] + 1)
                        p = PART if L1 else 2 * K0
                        dst = (keys(b % 2) + queries(b % 2))[i // 2 * 2][:, i % 2, :] if L1 else SH[0:p, 0, :].bitcast(F32R)
                        e.activation(dst, SL[0:p, i % 2, :], ACT.Copy).then_inc(hi_done, 1)

                    for P in range(-1, B):
                        ev = []
                        if P + 1 < B:
                            at = {(u, i): a for a, u, i, b in plan[P] if b == P + 1}
                            ev = [(2 if L1 else 0, 0, high, t) for t in range(CT)]
                            ev += [(at["qk", i] + 1 if P >= 0 else 3 + i, 1, qk_high, i) for i in range(NQK)]
                            ev.sort(key=lambda x: (x[0], x[1], x[3]))
                        if P >= 0:
                            for s in range(S):
                                if P or s >= 8:
                                    wait(e, av_done, S * P + s - 7)
                                    J = S * P + s - 8
                                    wait(e, sum_done, (NT - 1) * (J // NT) + max(J % NT, 1))
                                e.wait_ge(st_full, S * P + s + 1)
                                e.activation(pr_slot(s), psA[:, s % 2, :], ACT.Exp, scale=scale).then_inc(exp_done, 1)
                                while ev and ev[0][0] <= s:
                                    _, _, f, i = ev.pop(0)
                                    f(P + 1, i)
                        for _, _, f, i in ev:
                            f(P + 1, i)

                @block.gpsimd
                def _(e):
                    def rstd(b, _):
                        e.wait_ge(var_done, b + 1)
                        e.tensor_tensor(RSTD[:, :], VAR[:, :], MH[:, :], ALU.pow).then_inc(rstd_done, 1)

                    def low(b, t):
                        e.wait_ge(xh_done, CT * b + t + 1)
                        e.tensor_tensor(XL[:, t, :], SL[:, t, :] if L1 else X[:, b, t, :], XH[:, t, :].bitcast(F32),
                                        ALU.subtract).then_inc(xl_done, 1)

                    def qk_low(b, i):
                        e.wait_ge(hi_done, NQK * b + i + 1)
                        if L1:
                            hi, lo = [x[:, i % 2, :] for x in (keys, queries)[i // 2](b % 2)]
                            e.tensor_tensor(lo, SL[:, i % 2, :], hi.bitcast(F32), ALU.subtract).then_inc(lo_done, 1)
                        else:
                            p = 2 * K0
                            e.tensor_tensor(SL[0:p, 0, :].bitcast(F32R), SL[0:p, 0, :], SH[0:p, 0, :],
                                            ALU.subtract).then_inc(lo_done, 1)

                    def add(b, s):
                        h, j = s // NT, s % NT
                        e.wait_ge(exp_done, S * b + s + 1)
                        pa = PA[:, h * HALF:(h + 1) * HALF]
                        if j == 1:
                            if b:
                                e.wait_ge(d_full, index["sum", h, b - 1] + 1)
                        else:
                            e.wait_ge(sum_done, (NT - 1) * (2 * b + h) + j - 1)
                        e.tensor_tensor(pa, pr_slot(s - 1) if j == 1 else pa, pr_slot(s), ALU.add).then_inc(sum_done, 1)

                    for P in range(-1, B):
                        ev = []
                        if P >= 0:
                            ev += [(s, 2, add, P, s) for s in range(S) if s % NT]
                        if P + 1 < B:
                            at = {(u, i): a for a, u, i, b in plan[P] if b == P + 1}
                            if L1:
                                ev.append((0, 0, rstd, P + 1, 0))
                            ev += [(2 if L1 else 0, 1, low, P + 1, t) for t in range(CT)]
                            ev += [(at["qk", i] + 1 if P >= 0 else 3 + i, 3, qk_low, P + 1, i) for i in range(NQK)]
                        for _, _, f, b, i in sorted(ev, key=lambda x: (x[0], x[1], x[4])):
                            f(b, i)

                @block.sync
                def _(e):
                    for b in range(B):
                        if not L1:
                            e.wait_ge(lo_done, b + 1)
                            wait(e, st_full, S * (b - 1))
                            for dst, src in stack_copies(b % 2):
                                e.dma_start(dst, src).then_inc(stack_dma, 16)
                        e.wait_ge(d_free, index["T", 0, b] + 1)
                        if L1:
                            wait(e, st_full, S * b)
                            for i in range(2):
                                e.dma_start(MR1[i:i + 1, :], MRB[:, i, :]).then_inc(row_dma, 16)
                        else:
                            e.dma_start(QS[STACK:STACK + 1, b % 2, 0, :].bitcast(F32),
                                        MROW[0:NT, :].bitcast(F32)).then_inc(row_dma, 16)
                    e.wait_ge(row_dma, 16 * NROW * B)

        def stack_copies(slot):
            k, q = slice(0, K0), slice(K0, 2 * K0)
            for r, part in ((0, SH), (1, SL), (2, SH)):
                yield KS[r * K0:(r + 1) * K0, slot, 0, :].bitcast(F32), part[k, 0, :]
            for r, part in ((0, SH), (1, SH), (2, SL)):
                yield QS[r * K0:(r + 1) * K0, slot, 0, :].bitcast(F32), part[q, 0, :]

        def batch_norm():
            s_var, s_rstd, s_done = sem("bn_variance"), sem("bn_rstd"), sem("bn_done")
            with nc.Block() as block:
                @block.vector
                def _(e):
                    for t in range(CT):
                        for b in range(B):
                            for h in range(2):
                                e.bn_stats(BNS[:, t, 2 * b + h, :], X[:, b, t, h * HALF:(h + 1) * HALF])
                    e.drain()
                    for t in range(CT):
                        e.bn_aggr(MV[:, t, :], BNS[:, t].rearrange("p a b -> p (a b)"))
                    e.drain()
                    e.tensor_scalar(VAR[:, :], MV[:, :, 1], EPS, None, ALU.add).then_inc(s_var, 1)
                    e.wait_ge(s_rstd, 1)
                    norm_factors(e, 0, "bnw", "bnb")
                    for b in range(B):
                        for t in range(CT):
                            e.tensor_scalar(X[:, b, t, :], X[:, b, t, :], SC[:, 0, t, 0:1], SC[:, 0, t, 1:2],
                                            ALU.mult, ALU.add).then_inc(s_done, 1)
                    e.wait_ge(s_done, B * CT)

                @block.gpsimd
                def _(e):
                    e.wait_ge(s_var, 1)
                    e.tensor_tensor(RSTD[:, :], VAR[:, :], MH[:, :], ALU.pow).then_inc(s_rstd, 1)

        NGRP = B * GROUPS

        M_AT = (6, 55)
        STATS_AT, XN_AT = 3.6, 19
        KQ_AT = (38, 40.5)
        P_AT = (13, 16)

        def side_units(g, first):
            units = [("v", 0, 0), ("w", 3, 0)]
            if g == 0 and first:
                units = [("s", 0, 0), ("s", 0.1, 1), ("k", 0.5, 0), ("q", 0.6, 1), ("v", 1, 0), ("w", 2, 0)]
            if g == 1:
                units += [("s", 10, 0), ("s", 10.2, 1)]
                units += [] if first else [("p", P_AT[0], 0), ("p", P_AT[1], 1)]
            n = QUADH * NT
            units += [("m", M_AT[0] + i * (M_AT[1] - M_AT[0]) / n, i) for i in range(n)]
            units += [("K", KQ_AT[0], 0), ("Q", KQ_AT[1], 1), ("T", M_AT[1] + 1, 0)]
            return sorted(units, key=lambda x: x[1])

        def taken(units, k, engine):
            return sum((u in "vwkqKQ") == (engine == "scalar") for u, _, _ in units[:k])

        UNITS = [side_units(0, True), side_units(1, True), side_units(0, False), side_units(1, False)]
        BASE = {"all": [sum(len(u) for u in UNITS[:i]) for i in range(5)]}
        for _e in ("scalar", "vector"):
            BASE[_e] = [sum(taken(u, len(u), _e) for u in UNITS[:i]) for i in range(5)]
        LOOP = {k: v[4] - v[2] for k, v in BASE.items()}
        TAIL = {k: v[2] + LOOP[k] * (B - 1) for k, v in BASE.items()}
        assert BASE["all"][2] % 2 == 0 and LOOP["all"] % 2 == 0
        assert all(u[-1][0] == "T" and u[-2][0] == "m" for u in UNITS)

        def base_of(kind, place, r):
            return BASE[kind][place] if r is None else r * LOOP[kind] + BASE[kind][place]

        def units_taken(G, u):
            place, r = (G, None) if G < 2 else (2 + G % 2, G // 2 - 1)
            units = UNITS[place]
            return base_of("vector", place, r) + taken(units, [x[0] for x in units].index(u) + 1, "vector")

        WEIGH = [("av", 0, 12), ("av", 1, 13), ("av", 2, 15), ("av", 3, 18), ("av", 4, 22), ("av", 5, 25),
                 ("sum", 5, 26), ("av", 6, 29), ("sum", 6, 30), ("pa", NT, 32), ("av", 7, 34), ("sum", 7, 35)]
        assert [j for kind, j, _ in WEIGH if kind == "sum"] == list(range(NT - DIRECT, NT))
        HALF_STEPS = STEPS // 2
        TAKE_AT = 35.5

        def eight_heads(layer):
            load_weights(layer, 3 * C)
            scale = CH ** -0.5
            n = f"_{layer}"
            d_full = sem("unit_full" + n)
            vec_free, act_free = sem("unit_taken_by_vector" + n), sem("unit_taken_by_scalar" + n)
            st_full, exp_done = sem("scores_full" + n), sem("exp_done" + n)
            av_done, sum_done, out_done = sem("av_done" + n), sem("sum_done" + n), sem("out_done" + n)
            stat_done, var_done, rstd_done = sem("stat_done" + n), sem("var_done" + n), sem("rstd_done" + n)
            xn_done, xh_done, xl_done = sem("xn_done" + n), sem("xh_done" + n), sem("xl_done" + n)
            low_done, row_dma = sem("qk_low" + n), sem("max_row_filled" + n)
            stack_dma = [sem(f"stack_filled{n}_head{q}") for q in range(QUADH)]
            s_out = sem("stored" + n)

            def stacks_filled(e, G, heads=range(QUADH)):
                for q in heads:
                    wait(e, stack_dma[q], (G + 1) * STACK_DMAS * 16)

            with nc.Block() as block:
                @block.tensor
                def _(e):
                    def weigh(P, p, h, kind, j):
                        if kind == "pa":
                            wait(e, sum_done, ADDS * (2 * P + h + 1))
                        elif kind == "av":
                            if j == 0:
                                wait(e, out_done, 2 * P + h)
                            wait(e, exp_done, STEPS * P + QUADH * (NT * h + j + 1))
                        source = PA[:, :] if kind == "pa" else PR[:, j % 4, :]
                        source = source.rearrange("p (q n) -> p q n", q=QUADH)
                        for q in range(QUADH):
                            cols = slice(CH * q, CH * q + CH)
                            if kind == "av":
                                mm = e.matmul(psO[cols, 0, :], V[:, p, j, cols], source[:, q, :],
                                              start=(j == 0), stop=(j == NT - 1))
                            else:
                                mm = e.matmul(psO[cols, 1, :], ones[:, 0:CH], source[:, q, :],
                                              start=(j == NT - DIRECT), stop=(j == NT - 1))
                        if kind == ("sum" if j >= NT - DIRECT else "av"):
                            mm.then_inc(av_done, 1)

                    def all_taken(place, r, k):
                        engine = "scalar" if k > 0 and UNITS[place][k - 1][0] in "vwkqKQ" else "vector"
                        count = min(k, 0) + taken(UNITS[place], max(k, 0), engine)
                        wait(e, act_free if engine == "scalar" else vec_free, base_of(engine, place, r) + count)

                    def output(i, slot, group_halves, halves):
                        wait(e, out_done, group_halves)
                        return project_out(e, slot, i, halves)

                    def unit(place, r, k, G, g, t, halves=(0, 1)):
                        u, _, i = UNITS[place][k]
                        slot = (BASE["all"][place] + k) % 2
                        if 0 in halves and place + k >= 2:
                            all_taken(place, r, k - 1)
                        if u == "s":
                            wait(e, stat_done, t + 1)
                            mm = e.matmul(psD[:, slot, 0:2], gmat[:, :], GST[:, i, :], start=True, stop=True)
                        elif u in "kq":
                            if i == 0 and 0 in halves:
                                e.wait_ge(xh_done, CT)
                                e.wait_ge(xl_done, CT)
                            mm = project_in(e, slot, PART * i, PART, halves)
                        elif u in "KQ":
                            if i == 0 and 0 in halves:
                                wait(e, xh_done, G + 2 + g)
                                wait(e, xl_done, G + 2 + g)
                            mm = project_in(e, slot, 2 * PART * (1 - g) + PART * i, PART, halves)
                        elif u == "v":
                            mm = project_in(e, slot, 2 * C + PART * g, PART, halves)
                        elif u == "w":
                            all_taken(place, r, k)
                            for n in range(NT):
                                st = slice(n * PART, (n + 1) * PART)
                                mm = e.transpose(psD[:, slot, st], VT[:, st], ident[:, :])
                        elif u == "m":
                            q, tile = i // NT, i % NT
                            if tile == 0:
                                stacks_filled(e, G, [q])
                            for h in range(2):
                                mm = e.matmul(psD[:, slot, h * HALF:(h + 1) * HALF],
                                              QS[0:STACK, g, q, tile * PART:(tile + 1) * PART],
                                              KS[0:STACK, g, q, h * HALF:(h + 1) * HALF], start=True, stop=True)
                        elif u == "T":
                            all_taken(place, r, k)
                            mm = e.transpose(psD[0:QUADH * NT, slot, 0:PART], MX[:, :], ident[:, :])
                        elif u == "p":
                            mm = output(i, slot, t, halves)
                        if 1 in halves:
                            mm.then_inc(d_full, 1)

                    def phase(P, p, G, g, place, r=None, norm=None):
                        todo = []
                        for k, (u, at, i) in enumerate([] if G is None else UNITS[place]):
                            todo += ([(at, k, (0,)), (at + 1.2, k, (1,))] if u in "vKQp" else [(at, k, (0, 1))])

                        def next_unit():
                            _, k, halves = todo.pop(0)
                            unit(place, r, k, G, g, norm if UNITS[place][k][0] == "s" else None if P is None else P * 2, halves)

                        if P is None:
                            while todo:
                                next_unit()
                            return
                        wait(e, row_dma, (P + 1) * 16)
                        for s in range(STEPS):
                            h, j, q = s // (NT * QUADH), s // QUADH % NT, s % QUADH
                            wait(e, exp_done, STEPS * P + s - 1)
                            e.matmul(psA[:, s % 2, :], KS[0:STACK + 1, p, q, j * PART:(j + 1) * PART],
                                     QS[0:STACK + 1, p, q, h * HALF:(h + 1) * HALF],
                                     start=True, stop=True).then_inc(st_full, 1)
                            while todo and todo[0][0] <= s:
                                next_unit()
                            for kind, j, at in WEIGH:
                                if at + HALF_STEPS - STEPS == s and not (isinstance(P, int) and P == 0):
                                    weigh(P - 1, 1 - p, 1, kind, j)
                                for h in range(2):
                                    if at + HALF_STEPS * h == s:
                                        weigh(P, p, h, kind, j)

                    def tail():
                        for kind, j, at in WEIGH:
                            if at + HALF_STEPS >= STEPS:
                                weigh(NGRP - 1, 1, 1, kind, j)
                        for c in range(CT):
                            e.wait_ge(vec_free, TAIL["vector"] - 1 + c)
                            output(c, c % 2, 2 * NGRP, (0, 1)).then_inc(d_full, 1)

                    phase(None, None, 0, 0, 0, norm=0)
                    phase(0, 0, 1, 1, 1, norm=1)
                    with e.Fori(0, B - 1) as r:
                        phase(r * 2 + 1, 1, r * 2 + 2, 0, 2, r)
                        phase(r * 2 + 2, 0, r * 2 + 3, 1, 3, r, norm=r + 2)
                    phase(NGRP - 1, 1, None, None, 4)
                    tail()

                @block.vector
                def _(e):
                    def take_half(P, p, h):
                        wait(e, av_done, (2 * P + h + 1) * NT)
                        out_ap = A[:, p, h * HALF:(h + 1) * HALF]
                        e.reciprocal(out_ap, psO[:, 1, :])
                        e.drain()
                        e.tensor_tensor(out_ap, psO[:, 0, :], out_ap, ALU.mult).then_inc(out_done, 1)

                    def batch(b):
                        return X[:, b] if isinstance(b, int) else X[:, bass.ds(b, 1)].rearrange("p b t n -> p (b t) n")

                    def factors(b):
                        return SC[:, b] if isinstance(b, int) else SC[:, bass.ds(b, 1)].rearrange("p b t n -> p (b t) n")

                    def add_residual(c, b, full):
                        xb, sc = batch(b), factors(b)
                        if layer == 2:
                            e.tensor_scalar(xb[:, c, :], xb[:, c, :], sc[:, c, 0:1], sc[:, c, 1:2], ALU.mult, ALU.add)
                            e.drain()
                        return e.scalar_tensor_tensor(out=xb[:, c, :], in0=full, scalar=par(f"bp{layer}", 2)[:, c:c + 1],
                                                      in1=xb[:, c, :], op0=ALU.add, op1=ALU.add)

                    def normalise(norm, b, P, G):
                        e.wait_ge(rstd_done, norm + 1)
                        norm_factors_at(b)
                        if P is not None:
                            stacks_filled(e, G)
                        xb, sc = batch(b), factors(b)
                        for c in range(CT):
                            e.tensor_scalar(SL[:, c, :], xb[:, c, :], sc[:, c, 0:1], sc[:, c, 1:2],
                                            ALU.mult, ALU.add).then_inc(xn_done, 1)

                    def take(place, r, k, G, g, proj):
                        u, _, i = UNITS[place][k]
                        slot = (BASE["all"][place] + k) % 2
                        e.wait_ge(d_full, base_of("all", place, r) + k + 1)
                        full = psD[:, slot, :]
                        if u == "s":
                            e.tensor_copy(MV[:, i, :], psD[:, slot, 0:2]).then_inc(vec_free, 1)
                            if i == 1:
                                group_variance(e).then_inc(var_done, 1)
                        elif u == "m":
                            e.tensor_reduce(MX[:, i:i + 1], full, AX.X, ALU.max).then_inc(vec_free, 1)
                        elif u == "T":
                            wait(e, row_dma, G * 16)
                            e.tensor_scalar(MROW[:, :], psD[0:QUADH * NT, slot, 0:PART], -1.0, None,
                                            ALU.mult).then_inc(vec_free, 1)
                        else:
                            add_residual(i, proj, full).then_inc(vec_free, 1)

                    def phase(P, p, G, g, place, r=None, proj=None, norm=None, norm_b=None):
                        events = [(at, 0, k, "unit") for k, (u, at, i) in enumerate([] if G is None else UNITS[place])
                                  if u not in "vwkqKQ"]
                        if norm is not None:
                            events.append((-1 if P is None else STATS_AT, 0, 0, "stats"))
                            events.append((0.2 if P is None else XN_AT, 0, 0, "xn"))
                        if P is not None:
                            if not (isinstance(P, int) and P == 0):
                                events.append((TAKE_AT - HALF_STEPS, 0, 1, "half before"))
                            events.append((TAKE_AT, 0, 0, "half"))
                        for _, _, k, what in sorted(events):
                            if what == "half before":
                                take_half(P - 1, 1 - p, 1)
                            elif what == "half":
                                take_half(P, p, 0)
                            elif what == "stats":
                                norm_statistics(e, batch(norm_b)).then_inc(stat_done, 1)
                            elif what == "xn":
                                normalise(norm, norm_b, P, G)
                            else:
                                take(place, r, k, G, g, proj)

                    def norm_factors_at(b):
                        sc = factors(b)
                        e.tensor_tensor(sc[:, :, 0], RSTD[:, :], par(f"gw{layer}", 2), ALU.mult)
                        e.drain()
                        e.tensor_tensor(TMP[:, :], MV[:, :, 0], sc[:, :, 0], ALU.mult)
                        e.drain()
                        e.tensor_tensor(sc[:, :, 1], par(f"gb{layer}", 2), TMP[:, :], ALU.subtract)
                        e.drain()

                    phase(None, None, 0, 0, 0, norm=0, norm_b=0)
                    phase(0, 0, 1, 1, 1, norm=1, norm_b=1)
                    with e.Fori(0, B - 1) as r:
                        phase(r * 2 + 1, 1, r * 2 + 2, 0, 2, r)
                        phase(r * 2 + 2, 0, r * 2 + 3, 1, 3, r, proj=r, norm=r + 2, norm_b=(r + 2) % B)
                    phase(NGRP - 1, 1, None, None, 4)
                    take_half(NGRP - 1, 1, 1)
                    for c in range(CT):
                        e.wait_ge(d_full, TAIL["all"] + c + 1)
                        add_residual(c, B - 1, psD[:, c % 2, :]).then_inc(vec_free, 1)
                    e.drain()

                @block.scalar
                def _(e):
                    def run(what, k, place, r, G, g, norm):
                        if what == "x":
                            c = k
                            e.wait_ge(xn_done, CT * norm + c + 1)
                            if place:
                                used = [u for u, _, _ in UNITS[place]].index("v") + 1
                                e.wait_ge(d_full, base_of("all", place, r) + used)
                            e.activation(XH[:, c, :], SL[:, c, :], ACT.Copy).then_inc(xh_done, 1)
                            return
                        u, _, i = UNITS[place][k]
                        full = psD[:, (BASE["all"][place] + k) % 2, :]
                        e.wait_ge(d_full, base_of("all", place, r) + k + 1)
                        if u == "v":
                            e.activation(VT[:, :], full, ACT.Identity,
                                         bias=par(f"bv{layer}", 2)[:, g:g + 1]).then_inc(act_free, 1)
                        elif u == "w":
                            wait(e, av_done, (G - 1) * 2 * NT)
                            e.activation(V[:, g, :, :].rearrange("p t c -> p (t c)"), full, ACT.Copy).then_inc(act_free, 1)
                        else:
                            if u in "KQ":
                                stacks_filled(e, G)
                            column = 2 * (g if u in "kq" else 1 - g) + i
                            bias = par(f"bqk{layer}", 4)[:, column:column + 1]
                            e.activation(SH[:, i, :].bitcast(F32R), full, ACT.Identity, bias=bias)
                            e.activation(SL[:, i, :], full, ACT.Identity, bias=bias).then_inc(act_free, 1)

                    def phase(P, p, G, g, place, r=None, norm=None):
                        wide = {"v": 2, "w": 1, "k": 0, "q": 0, "K": 2, "Q": 2}
                        events = [(int(at) + wide[u], "unit", k) for k, (u, at, i) in enumerate([] if G is None else UNITS[place])
                                  if u in wide]
                        if norm is not None:
                            events += [(-1 if P is None else XN_AT + 4 + 3 * c, "x", c) for c in range(CT)]
                        events.sort()

                        if P is None:
                            for x in events:
                                run(*x[1:], place, r, G, g, norm)
                            return
                        for s in range(STEPS):
                            J = s // QUADH
                            if s % QUADH == 0:
                                if J >= 4:
                                    wait(e, av_done, 2 * NT * P + J - 3)
                                    h, j = (J - 4) // NT, (J - 4) % NT
                                    wait(e, sum_done, ADDS * (2 * P + h) + min(max(j, 1), ADDS))
                                else:
                                    wait(e, av_done, 2 * NT * P + J - 3)
                                    wait(e, sum_done, ADDS * 2 * P)
                            wait(e, st_full, STEPS * P + s + 1)
                            e.activation(PR[:, J % 4, (s % QUADH) * HALF:(s % QUADH + 1) * HALF], psA[:, s % 2, :],
                                         ACT.Exp, scale=scale).then_inc(exp_done, 1)
                            while events and events[0][0] <= s:
                                run(*events.pop(0)[1:], place, r, G, g, norm)

                    phase(None, None, 0, 0, 0, norm=0)
                    phase(0, 0, 1, 1, 1, norm=1)
                    with e.Fori(0, B - 1) as r:
                        phase(r * 2 + 1, 1, r * 2 + 2, 0, 2, r)
                        phase(r * 2 + 2, 0, r * 2 + 3, 1, 3, r, norm=r + 2)
                    phase(NGRP - 1, 1, None, None, 4)

                @block.gpsimd
                def _(e):
                    def rstd(norm):
                        e.wait_ge(var_done, norm + 1)
                        e.tensor_tensor(RSTD[:, :], VAR[:, :], MH[:, :], ALU.pow).then_inc(rstd_done, 1)

                    def input_low(norm):
                        for c in range(CT):
                            e.wait_ge(xh_done, CT * norm + c + 1)
                            e.tensor_tensor(XL[:, c, :], SL[:, c, :], XH[:, c, :].bitcast(F32),
                                            ALU.subtract).then_inc(xl_done, 1)

                    def low(place, r, u, k):
                        units = UNITS[place]
                        e.wait_ge(act_free, base_of("scalar", place, r)
                                  + taken(units, [x[0] for x in units].index(u) + 1, "scalar"))
                        e.tensor_tensor(SL[:, k, :].bitcast(F32R), SL[:, k, :], SH[:, k, :],
                                        ALU.subtract).then_inc(low_done, 1)

                    def phase(P, place, r=None, norm=None):
                        if P is None:
                            rstd(norm)
                            input_low(norm)
                            for k in range(2):
                                low(place, r, "kq"[k], k)
                            for k in range(2):
                                low(place, r, "KQ"[k], k)
                            return
                        for h in range(2):
                            for j in range(1, ADDS + 1):
                                J = h * NT + j
                                wait(e, exp_done, STEPS * P + QUADH * (J + 1))
                                if j == 1:
                                    wait(e, av_done, NT * (2 * P + h))
                                else:
                                    wait(e, sum_done, ADDS * (2 * P + h) + j - 1)
                                e.tensor_tensor(PA[:, :], PR[:, (J - 1) % 4, :] if j == 1 else PA[:, :],
                                                PR[:, J % 4, :], ALU.add).then_inc(sum_done, 1)
                                if norm is not None and h == 0 and j == 2:
                                    rstd(norm)
                                if place < 4 and h == 1 and j <= 2:
                                    low(place, r, "KQ"[j - 1], j - 1)
                            if norm is not None and h == 0:
                                input_low(norm)

                    phase(None, 0, norm=0)
                    phase(0, 1, norm=1)
                    with e.Fori(0, B - 1) as r:
                        phase(r * 2 + 1, 2, r)
                        phase(r * 2 + 2, 3, r, norm=r + 2)
                    phase(NGRP - 1, 4)

                @block.sync
                def _(e):
                    for G in range(NGRP):
                        g = G % 2
                        e.wait_ge(low_done, 2 * (G + 1))
                        wait(e, st_full, STEPS * (G - 1))
                        for q in range(QUADH):
                            rows = slice(CH * q, CH * (q + 1))
                            for r in range(3):
                                dst = slice(CH * r, CH * (r + 1))
                                e.dma_start(KS[dst, g, q, :].bitcast(F32),
                                            (SH, SL, SH)[r][rows, 0, :]).then_inc(stack_dma[q], 16)
                                e.dma_start(QS[dst, g, q, :].bitcast(F32),
                                            (SH, SH, SL)[r][rows, 1, :]).then_inc(stack_dma[q], 16)
                        if layer == 3 and g == 0 and G >= 4:
                            b = G // 2 - 2
                            e.dma_start(out_v[:, b], X[:, b]).then_inc(s_out, 16)
                        e.wait_ge(vec_free, units_taken(G, "T"))
                        e.dma_start(QS[STACK:STACK + 1, g, :, :].rearrange("p q n -> p (q n)").bitcast(F32),
                                    MROW[:, :].bitcast(F32)).then_inc(row_dma, 16)
                    if layer == 3:
                        e.dma_start(out_v[:, B - 2], X[:, B - 2]).then_inc(s_out, 16)
                        e.wait_ge(vec_free, TAIL["vector"] + CT)
                        e.dma_start(out_v[:, B - 1], X[:, B - 1]).then_inc(s_out, 16)
                        e.wait_ge(s_out, 16 * B)

        single_head(0)
        batch_norm()
        single_head(1)
        eight_heads(2)
        eight_heads(3)


def laid_out(inputs):
    import numpy as np

    f = {k: np.asarray(v) for k, v in inputs.items()}
    ident = np.eye(PART, dtype=np.float32)
    gmat = np.kron(np.eye(PART // 8), np.full((8, 8), 1 / 8)).astype(np.float32)
    par = np.zeros((PART, NPAR), np.float32)

    def put(name, v):
        v = np.asarray(v).reshape(-1)
        for i in range(max(1, len(v) // PART)):
            w = v[i * PART:(i + 1) * PART]
            par[:len(w), PC[name] + i] = w

    par[:, PC["gamma0"]] = f["L0_conv_gamma"]
    put("bnw", f["L0_conv_bn_w"])
    put("bnb", f["L0_conv_bn_b"])
    put("bqk0", np.concatenate([f["L0_conv_bk"], f["L0_conv_bq"]]))
    w, bv, wp = [], [], []
    w.append(np.concatenate([f["L0_conv_Wk"], f["L0_conv_Wq"], f["L0_conv_Wv"]]))
    bv.append(f["L0_conv_bv"])
    order = np.concatenate([np.arange(C, 2 * C), np.arange(C), np.arange(2 * C, 3 * C)])
    orders = {1: order}
    rows = np.arange(3 * C).reshape(HEADS, 3, CH)
    parts = [rows[g * QUADH:(g + 1) * QUADH, k].reshape(-1) for g in range(GROUPS) for k in (1, 0)]
    orders[2] = orders[3] = np.concatenate(parts + [rows[:, 2].reshape(-1)])
    norm = {1: ("gamma", "beta"), 2: ("gn_w", "gn_b"), 3: ("norm_scale", "norm_bias")}
    for n in (1, 2, 3):
        pre = f"L{n}_conv_"
        wl, bl = f[pre + "qkv_w"][orders[n]], f[pre + "qkv_b"][orders[n]]
        w.append(wl)
        bv.append(bl[2 * C:])
        wp.append(f[pre + "proj_w"])
        put(f"gw{n}", f[pre + norm[n][0]])
        put(f"gb{n}", f[pre + norm[n][1]])
        put(f"bp{n}", f[pre + "proj_b"])
        put(f"bv{n}", bl[2 * C:])
        put(f"bqk{n}", bl[:2 * C])
    arrays = {"x": np.ascontiguousarray(f["x"].reshape(B, C, N))}
    for n in range(4):
        arrays[f"w{n}"] = np.ascontiguousarray(w[n].T)
    for n in (1, 2, 3):
        arrays[f"wp{n}"] = np.ascontiguousarray(wp[n - 1].T)
    for n in range(2):
        arrays[f"bv{n}"] = np.ascontiguousarray(np.broadcast_to(bv[n], (PART, C)))
    arrays |= {"par": par, "ident": ident, "gmat": gmat}
    return arrays


def kernel(**inputs):
    import concourse.bacc as bacc
    from concourse.bass_utils import run_bass_kernel_spmd

    nc = bacc.Bacc("TRN2", target_bir_lowering=False, num_devices=1)
    arrays = laid_out(inputs)
    args = [nc.dram_tensor(k, a.shape, mybir.dt.from_np(a.dtype), kind="ExternalInput").ap() for k, a in arrays.items()]
    args.append(nc.dram_tensor("out", (B, C, N), F32, kind="ExternalOutput").ap())
    attention_stack(nc, *args)
    r = run_bass_kernel_spmd(nc, [arrays], core_ids=[0])
    return r.results[0]["out"].reshape(B, C, 32, 32)
```

```python
from contextlib import ExitStack

import concourse.bass as bass
from concourse import mybir

ALU = mybir.AluOpType
ACT = mybir.ActivationFunctionType
AX = mybir.AxisListType
F32 = mybir.dt.float32
F32R = mybir.dt.float32r
BF16 = mybir.dt.bfloat16

B, C, N = 4, 256, 1024
PART = 128
CT = C // PART
NT = N // PART
HALF = N // 2
HEADS, CH = 8, 32
QUADH = 4
GROUPS = HEADS // QUADH
K0 = C // 8
STACK = 3 * CH
EPS = 1e-5

STEPS = 2 * NT * QUADH
DIRECT = 2
ADDS = NT - DIRECT - 1
STACK_DMAS = 6

PC = {"gamma0": 0, "bnw": 1, "bnb": 3, "bqk0": 5}
for _n, _l in enumerate((1, 2, 3)):
    for _k, _f in enumerate(("gw", "gb", "bp", "bv", "bqk")):
        PC[f"{_f}{_l}"] = 6 + 12 * _n + 2 * _k
NPAR = 6 + 12 * 3


def attention_stack(nc, x, w0, w1, w2, w3, wp1, wp2, wp3, bv0, bv1, par_d, ident_d, gmat_d, out):
    with ExitStack() as ctx:
        def sb(name, shape, dt=F32):
            return ctx.enter_context(nc.sbuf_tensor(name, shape, dt))

        def sem(name):
            return ctx.enter_context(nc.semaphore(name))

        X = sb("X", [PART, B, CT, N])
        XH = sb("XH", [PART, CT, N], F32R)
        XL = sb("XL", [PART, CT, N], F32R)
        SH = sb("SH", [PART, 2, N])
        SL = sb("SL", [PART, 2, N])
        KS = sb("KS", [PART, 2, QUADH, N], F32R)
        QS = sb("QS", [PART, 2, QUADH, N], F32R)
        V = sb("V", [PART, GROUPS, NT, PART])
        PR = sb("PR", [PART, 4, QUADH * HALF])
        PA = sb("PA", [PART, QUADH * HALF])
        A = sb("A", [PART, CT, N])
        WH = sb("WH", [PART, CT, 3 * C], F32R)
        WL = sb("WL", [PART, CT, 3 * C], F32R)
        WP = sb("WP", [PART, CT, C])
        VT = sb("VT", [PART, N])
        BV = VT[:, 0:C]
        PAR = sb("PAR", [PART, NPAR])
        ident = sb("identity", [PART, PART])
        gmat = sb("group_mean", [PART, PART])
        ones = sb("ones", [PART, PART])
        MX = sb("MX", [PART, 32])
        MROW = sb("MROW", [32, PART], F32R)
        BST = sb("BST", [PART, CT, 2, 6])
        MV = sb("MV", [PART, CT, 2])
        GST = sb("GST", [PART, CT, 2])
        VAR = sb("VAR", [PART, CT])
        RSTD = sb("RSTD", [PART, CT])
        MH = sb("MH", [PART, CT])
        SC = sb("SC", [PART, B, CT, 2])
        BNS = sb("BNS", [PART, CT, B * 2, 6])
        MXH = BNS[:, :, :, :].rearrange("p a b c -> p (a b c)")[:, 0:2 * 32].rearrange("p (h q t) -> p h q t", h=2, q=QUADH)
        TMP = sb("TMP", [PART, CT])
        ONEB = sb("ONEB", [PART, PART], BF16)
        MRB = sb("MRB", [NT, 2, PART], BF16)
        MR1 = sb("MR1", [PART, N], BF16)

        psD = ctx.enter_context(nc.psum_tensor("psD", [PART, 2, N], F32))
        psA = ctx.enter_context(nc.psum_tensor("psA", [PART, 2, HALF], F32))
        psO = ctx.enter_context(nc.psum_tensor("psO", [PART, 2, HALF], F32))

        def par(name, n=1, p=PART):
            return PAR[0:p, PC[name]:PC[name] + n]

        x_v = x.rearrange("b (t p) n -> p b t n", p=PART)
        out_v = out.rearrange("b (t p) n -> p b t n", p=PART)
        w_dram = [w.rearrange("(t p) n -> p t n", p=PART) for w in (w0, w1, w2, w3)]
        wp_dram = [None] + [w.rearrange("(t p) n -> p t n", p=PART) for w in (wp1, wp2, wp3)]
        bv_dram = [bv0, bv1]

        WIDE = (2 * K0 + C, 3 * C, 3 * C)
        x_loaded = [sem(f"x_loaded_{b}") for b in range(B)]
        w_loaded = [sem(f"w_loaded_{layer}") for layer in range(3)]
        bv_loaded = [sem(f"bv_loaded_{layer}") for layer in range(2)]
        wp_loaded = [None] + [sem(f"wp_loaded_{layer}") for layer in (1, 2, 3)]

        def raw_weights(layer):
            return PR[:, 3, 0:CT * WIDE[layer]].rearrange("p (t n) -> p t n", t=CT)

        s_const, s_memset = sem("constants_loaded"), sem("memsets_done")
        with nc.Block() as block:
            @block.sync
            def _(e):
                e.dma_start(raw_weights(0), w_dram[0]).then_inc(w_loaded[0], 16)
                e.dma_start(X[:, 0], x_v[:, 0]).then_inc(x_loaded[0], 16)
                for tile, d in ((PAR, par_d), (ident, ident_d), (gmat, gmat_d)):
                    e.dma_start(tile[:, :], d).then_inc(s_const, 16)
                e.dma_start(BV, bv_dram[0]).then_inc(bv_loaded[0], 16)
                for b in range(1, B):
                    e.dma_start(X[:, b], x_v[:, b]).then_inc(x_loaded[b], 16)

            @block.vector
            def _(e):
                e.memset(ones[:, :], 1.0).then_inc(s_memset, 1)
                e.memset(MH[:, :], -0.5).then_inc(s_memset, 1)
                e.memset(KS[STACK:STACK + 1].bitcast(F32), 1.0).then_inc(s_memset, 1)
                e.memset(ONEB[:, :], 0.0).then_inc(s_memset, 1)
                e.memset(MR1[:, :], 0.0).then_inc(s_memset, 1)
                e.drain()
                e.memset(ONEB[0:2, :], 1.0).then_inc(s_memset, 1)
                e.wait_ge(s_memset, 6)
                e.wait_ge(s_const, 48)

        def split_weights(layer):
            w_high, w_split = sem(f"w_high_{layer}"), sem(f"w_split_{layer}")
            raw, wide = raw_weights(layer), WIDE[layer]
            with nc.Block() as block:
                @block.sync
                def _(e):
                    if layer == 1:
                        e.dma_start(BV, bv_dram[1]).then_inc(bv_loaded[1], 16)
                    if layer:
                        e.dma_start(WP[:, :, :], wp_dram[layer]).then_inc(wp_loaded[layer], 16)
                    if layer < 2:
                        e.wait_ge(w_split, 1)
                        e.dma_start(raw_weights(layer + 1), w_dram[layer + 1]).then_inc(w_loaded[layer + 1], 16)

                @block.vector
                def _(e):
                    e.wait_ge(w_loaded[layer], 16)
                    e.tensor_copy(WH[:, :, 0:wide], raw).then_inc(w_high, 1)
                    e.wait_ge(w_high, 1)
                    e.tensor_tensor(WL[:, :, 0:wide], raw, WH[:, :, 0:wide], ALU.subtract).then_inc(w_split, 1)
                    e.wait_ge(w_split, 1)
                    if layer < 2:
                        e.wait_ge(bv_loaded[layer], 16)

                @block.gpsimd
                def _(e):
                    if layer == 2:
                        e.memset(KS[STACK:STACK + 1].bitcast(F32), 1.0)

        def split_products(e, out_ap, terms):
            last = None
            for i, (w, m) in enumerate(terms):
                last = e.matmul(out_ap, w, m, start=(i == 0), stop=(i == len(terms) - 1))
            return last

        def project_in(e, slot, col, width):
            for h in range(2):
                mv = slice(h * HALF, (h + 1) * HALF)
                terms = [(w[:, t, col:col + width], xx[:, t, mv])
                         for w, xx in ((WH, XH), (WL, XH), (WH, XL)) for t in range(CT)]
                last = split_products(e, psD[0:width, slot, mv], terms)
            return last

        def project_values(e, slot, col, i):
            for n in range(NT // 2):
                st = slice((NT // 2 * i + n) * PART, (NT // 2 * i + n + 1) * PART)
                terms = [(xx[:, t, st], w[:, t, col:col + C])
                         for xx, w in ((XH, WH), (XL, WH), (XH, WL)) for t in range(CT)]
                last = split_products(e, psD[:, slot, n * C:(n + 1) * C], terms)
            return last

        def project_out(e, slot, o):
            for h in range(2):
                mv = slice(h * HALF, (h + 1) * HALF)
                last = split_products(e, psD[:, slot, mv],
                                      [(WP[:, t, o * PART:(o + 1) * PART], A[:, t, mv]) for t in range(CT)])
            return last

        def values_of(slot):
            return V[:, :, :, :] if slot == 0 else PR[:, 2, :].rearrange("p (g t c) -> p g t c", g=CT, t=NT)

        def bias_values(e, slot, vslot, i):
            out_ap = values_of(vslot).rearrange("p g t c -> p t g c")[:, NT // 2 * i:NT // 2 * (i + 1)]
            full = psD[:, slot, :].rearrange("p (t g c) -> p t g c", t=NT // 2, g=CT)
            bias = BV.rearrange("p (g c) -> p g c", g=CT).unsqueeze(1).broadcast_to((PART, NT // 2, CT, PART))
            return e.tensor_tensor(out_ap, full, bias, ALU.add)

        def norm_statistics(e, xb):
            for t in range(CT):
                for h in range(2):
                    e.bn_stats(BST[:, t, h, :], xb[:, t, h * HALF:(h + 1) * HALF])
            e.drain()
            for t in range(CT):
                e.bn_aggr(MV[:, t, :], BST[:, t, :, :].rearrange("p a b -> p (a b)"))
            e.drain()
            e.tensor_tensor(GST[:, :, 1], MV[:, :, 0], MV[:, :, 0], ALU.mult)
            e.drain()
            e.tensor_tensor(GST[:, :, 1], GST[:, :, 1], MV[:, :, 1], ALU.add)
            return e.tensor_copy(GST[:, :, 0], MV[:, :, 0])

        def group_variance(e):
            e.drain()
            e.tensor_tensor(TMP[:, :], MV[:, :, 0], MV[:, :, 0], ALU.mult)
            e.drain()
            e.tensor_tensor(TMP[:, :], MV[:, :, 1], TMP[:, :], ALU.subtract)
            e.drain()
            return e.tensor_scalar(VAR[:, :], TMP[:, :], EPS, None, ALU.add)

        def norm_factors(e, b, gw, gb):
            e.tensor_tensor(SC[:, b, :, 0], RSTD[:, :], par(gw, 2), ALU.mult)
            e.drain()
            e.tensor_tensor(TMP[:, :], MV[:, :, 0], SC[:, b, :, 0], ALU.mult)
            e.drain()
            e.tensor_tensor(SC[:, b, :, 1], par(gb, 2), TMP[:, :], ALU.subtract)
            e.drain()

        def wait(e, s, value):
            if not isinstance(value, int) or value > 0:
                e.wait_ge(s, value)

        WEIGH_AT = [4, 4, 5, 5, 6, 7, 8, 9]

        def single_head(layer):
            split_weights(layer)
            L1 = layer == 1
            vcol = WIDE[layer] - C
            scale = 1.0 if layer == 0 else C ** -0.5
            NQK = 4 if L1 else 1
            NSTACK = 6
            NROW = 2 if L1 else 1
            S = 2 * NT
            n = f"_{layer}"
            d_full, d_free = sem("unit_full" + n), sem("unit_free" + n)
            st_full, exp_done = sem("scores_full" + n), sem("exp_done" + n)
            av_done, sum_done, out_done = sem("av_done" + n), sem("sum_done" + n), sem("out_done" + n)
            stat_done, var_done, rstd_done = sem("stat_done" + n), sem("var_done" + n), sem("rstd_done" + n)
            xn_done, xh_done, xl_done = sem("xn_done" + n), sem("xh_done" + n), sem("xl_done" + n)
            hi_done, lo_done = sem("qk_high" + n), sem("qk_low" + n)
            stack_dma, row_dma = sem("stack_filled" + n), sem("max_row_filled" + n)

            prep = ([("s", 0)] if L1 else []) + [("qk", i) for i in range(NQK)] + [("v", 0), ("v", 1)]
            prep += [("m", i) for i in range(NT)] + [("T", 0)]
            if L1:
                prep_at = [1, 5, 5, 6, 6, 7, 8, 10, 10, 11, 11, 12, 12, 13, 13, 14]
            else:
                prep_at = [3, 4, 5, 7, 8, 8, 9, 11, 11, 12, 12, 14]
            plan = {}
            index = {}
            for P in range(-1, B + 1):
                ev = []
                if P + 1 < B:
                    ev += [(at if P >= 0 else -1, k, u, i, P + 1) for k, ((u, i), at) in enumerate(zip(prep, prep_at))]
                if 0 <= P < B:
                    ev.append((9 if L1 else 10, -1, "sum", 0, P))
                if P > 0:
                    ev.append((1 if L1 else 2, -1, "sum", 1, P - 1))
                    if L1:
                        ev += [(4, -1, "p", c, P - 1) for c in range(CT)]
                plan[P] = [(at, u, i, b) for at, _, u, i, b in sorted(ev, key=lambda x: (x[0], x[1], x[3]))]
                for _, u, i, b in plan[P]:
                    index[u, i, b] = len(index)

            def keys(slot):
                return KS[:, slot, 0:2], KS[:, slot, 2:4]

            def queries(slot):
                return QS[:, slot, 0:2], QS[:, slot, 2:4]

            def pr_slot(s):
                return PR[:, s % 8 // 4, (s % 4) * HALF:(s % 4 + 1) * HALF]

            with nc.Block() as block:
                @block.tensor
                def _(e):
                    def unit(u, i, b):
                        k = index[u, i, b]
                        slot, buf = k % 2, b % 2
                        wait(e, d_free, k - 1)
                        if u == "s":
                            e.wait_ge(stat_done, b + 1)
                            mm = e.matmul(psD[:, slot, 0:4], gmat[:, :], GST[:, :, :].rearrange("p a b -> p (a b)"),
                                          start=True, stop=True)
                        elif u == "qk":
                            if i == 0:
                                e.wait_ge(xh_done, CT * (b + 1))
                                e.wait_ge(xl_done, CT * (b + 1))
                            mm = project_in(e, slot, PART * i, PART if L1 else 2 * K0)
                        elif u == "v":
                            mm = project_values(e, slot, vcol, i)
                        elif u == "m":
                            tile = slice(i * PART, (i + 1) * PART)
                            if i == 0:
                                if L1:
                                    e.wait_ge(hi_done, NQK * (b + 1))
                                else:
                                    e.wait_ge(stack_dma, 16 * NSTACK * (b + 1))
                            for h in range(2):
                                mv = slice(h * HALF, (h + 1) * HALF)
                                terms = ([(queries(buf)[0][:, t, tile], keys(buf)[0][:, t, mv]) for t in range(CT)] if L1
                                         else [(QS[0:STACK, buf, 0, tile], KS[0:STACK, buf, 0, mv])])
                                mm = split_products(e, psD[:, slot, mv], terms)
                        elif u == "T":
                            e.wait_ge(d_free, k)
                            mm = e.transpose(psD[0:NT, slot, 0:PART], MX[:, 0:NT], ident[:, :])
                        elif u == "sum":
                            e.wait_ge(sum_done, (NT - 1) * (2 * b + i + 1))
                            mm = e.matmul(psD[:, slot, 0:HALF], ones[:, :], PA[:, i * HALF:(i + 1) * HALF],
                                          start=True, stop=True)
                        else:
                            e.wait_ge(out_done, 2 * (b + 1))
                            e.wait_ge(wp_loaded[1], 16)
                            mm = project_out(e, slot, i)
                        mm.then_inc(d_full, 1)

                    def scores(P, s):
                        h, j = s // NT, s % NT
                        mv, tile = slice(h * HALF, (h + 1) * HALF), slice(j * PART, (j + 1) * PART)
                        wait(e, exp_done, S * P + s - 1)
                        if L1:
                            (kh, kl), (qh, ql) = keys(P % 2), queries(P % 2)
                            for i, (kk, qq) in enumerate(((kh, qh), (kl, qh), (kh, ql))):
                                for t in range(CT):
                                    e.matmul(psA[:, s % 2, :], kk[:, t, tile], qq[:, t, mv], start=(i == t == 0), stop=False)
                            mm = e.matmul(psA[:, s % 2, :], ONEB[:, :], MR1[:, mv], start=False, stop=True)
                        else:
                            mm = e.matmul(psA[:, s % 2, :], KS[0:STACK + 1, P % 2, 0, tile],
                                          QS[0:STACK + 1, P % 2, 0, mv], start=True, stop=True)
                        mm.then_inc(st_full, 1)

                    def weigh(P, s):
                        h, j = s // NT, s % NT
                        if j == 0:
                            wait(e, out_done, 2 * P + h)
                        e.wait_ge(exp_done, S * P + s + 1)
                        for t in range(CT):
                            mm = e.matmul(psO[:, t, :], values_of(P % 2)[:, t, j, :], pr_slot(s),
                                          start=(j == 0), stop=(j == NT - 1))
                        mm.then_inc(av_done, 1)

                    for P in range(-1, B + 1):
                        todo = list(plan[P])
                        if 0 <= P < B:
                            e.wait_ge(row_dma, 16 * NROW * (P + 1))
                            if L1:
                                e.wait_ge(lo_done, NQK * (P + 1))
                            for s in range(S):
                                scores(P, s)
                                for x in range(S):
                                    if WEIGH_AT[x % NT] + NT * (x // NT) == s + S and P > 0:
                                        weigh(P - 1, x)
                                for x in range(S):
                                    if WEIGH_AT[x % NT] + NT * (x // NT) == s:
                                        weigh(P, x)
                                while todo and todo[0][0] <= s:
                                    unit(*todo.pop(0)[1:])
                        elif P == B:
                            weigh(B - 1, S - 2)
                            weigh(B - 1, S - 1)
                        for x in todo:
                            unit(*x[1:])

                @block.vector
                def _(e):
                    for P in range(-1, B + 1):
                        stats_left = L1 and P + 1 < B
                        if stats_left:
                            for t in range(CT):
                                e.tensor_scalar(X[:, P + 1, t, :], X[:, P + 1, t, :], SC[:, 1, t, 0:1], SC[:, 1, t, 1:2],
                                                ALU.mult, ALU.add)
                            e.drain()
                            norm_statistics(e, X[:, P + 1]).then_inc(stat_done, 1)
                        for _, u, i, b in plan[P]:
                            k = index[u, i, b]
                            slot = k % 2
                            full = psD[:, slot, :]
                            e.wait_ge(d_full, k + 1)
                            if u == "s":
                                e.tensor_copy(MV[:, :, :].rearrange("p a b -> p (a b)"), psD[:, slot, 0:4]).then_inc(d_free, 1)
                                group_variance(e).then_inc(var_done, 1)
                                e.wait_ge(rstd_done, b + 1)
                                norm_factors(e, 0, "gw1", "gb1")
                                wait(e, lo_done, NQK * b)
                                for t in range(CT):
                                    e.tensor_scalar(SL[:, t, :], X[:, b, t, :], SC[:, 0, t, 0:1], SC[:, 0, t, 1:2],
                                                    ALU.mult, ALU.add).then_inc(xn_done, 1)
                            elif u == "qk":
                                if i >= 2:
                                    e.wait_ge(lo_done, NQK * b + i - 1)
                                if not L1:
                                    wait(e, stack_dma, 16 * NSTACK * b)
                                p = PART if L1 else 2 * K0
                                e.tensor_scalar(SL[0:p, i % 2, :], full[0:p, :],
                                                par("bqk1", 4)[:, i:i + 1] if L1 else par("bqk0", 1, p),
                                                None, ALU.add).then_inc(d_free, 1)
                            elif u == "v":
                                wait(e, av_done, S * (b - 1))
                                bias_values(e, slot, b % 2, i).then_inc(d_free, 1)
                            elif u == "m":
                                e.tensor_reduce(MX[:, i:i + 1], full, AX.X, ALU.max).then_inc(d_free, 1)
                            elif u == "T":
                                wait(e, row_dma, 16 * NROW * b)
                                top = psD[0:NT, slot, 0:PART]
                                if L1:
                                    e.tensor_scalar(MRB[:, 0, :], top, -1.0, None, ALU.mult)
                                    e.drain()
                                    e.scalar_tensor_tensor(out=MRB[:, 1, :], in0=top, scalar=-1.0, in1=MRB[:, 0, :],
                                                           op0=ALU.mult, op1=ALU.subtract).then_inc(d_free, 1)
                                else:
                                    e.tensor_scalar(MROW[0:NT, :], top, -1.0, None, ALU.mult).then_inc(d_free, 1)
                            elif u == "sum":
                                mv = slice(i * HALF, (i + 1) * HALF)
                                e.reciprocal(VT[:, HALF:N], psD[:, slot, 0:HALF]).then_inc(d_free, 1)
                                e.drain()
                                e.wait_ge(av_done, S * b + NT * (i + 1))
                                for t in range(CT):
                                    mul = e.tensor_tensor(A[:, t, mv], psO[:, t, :], VT[:, HALF:N], ALU.mult)
                                mul.then_inc(out_done, 1)
                                e.drain()
                                if not L1:
                                    for t in range(CT):
                                        e.scalar_tensor_tensor(out=X[:, b, t, mv], in0=A[:, t, mv], scalar=par("gamma0"),
                                                               in1=X[:, b, t, mv], op0=ALU.mult, op1=ALU.add)
                                    e.drain()
                                    for t in range(CT):
                                        e.bn_stats(BNS[:, t, 2 * b + i, :], X[:, b, t, mv])
                            else:
                                e.scalar_tensor_tensor(out=X[:, b, i, :], in0=full, scalar=par("bp1", 2)[:, i:i + 1],
                                                       in1=X[:, b, i, :], op0=ALU.add, op1=ALU.add).then_inc(d_free, 1)
                    e.drain()

                @block.scalar
                def _(e):
                    def high(b, t):
                        if L1:
                            e.wait_ge(xn_done, CT * b + t + 1)
                            src = SL[:, t, :]
                        else:
                            e.wait_ge(x_loaded[b], 16)
                            src = X[:, b, t, :]
                        if b:
                            e.wait_ge(d_full, index["v", 1, b - 1] + 1)
                        e.activation(XH[:, t, :], src, ACT.Copy).then_inc(xh_done, 1)

                    def qk_high(b, i):
                        e.wait_ge(d_free, index["qk", i, b] + 1)
                        p = PART if L1 else 2 * K0
                        dst = (keys(b % 2) + queries(b % 2))[i // 2 * 2][:, i % 2, :] if L1 else SH[0:p, 0, :].bitcast(F32R)
                        e.activation(dst, SL[0:p, i % 2, :], ACT.Copy).then_inc(hi_done, 1)

                    for P in range(-1, B):
                        ev = []
                        if P + 1 < B:
                            at = {(u, i): a for a, u, i, b in plan[P] if b == P + 1}
                            ev = [(2 if L1 else 0, 0, high, t) for t in range(CT)]
                            ev += [(at["qk", i] + 1 if P >= 0 else 3 + i, 1, qk_high, i) for i in range(NQK)]
                            ev.sort(key=lambda x: (x[0], x[1], x[3]))
                        if P >= 0:
                            for s in range(S):
                                if P or s >= 8:
                                    wait(e, av_done, S * P + s - 7)
                                    J = S * P + s - 8
                                    wait(e, sum_done, (NT - 1) * (J // NT) + max(J % NT, 1))
                                e.wait_ge(st_full, S * P + s + 1)
                                e.activation(pr_slot(s), psA[:, s % 2, :], ACT.Exp, scale=scale).then_inc(exp_done, 1)
                                while ev and ev[0][0] <= s:
                                    _, _, f, i = ev.pop(0)
                                    f(P + 1, i)
                        for _, _, f, i in ev:
                            f(P + 1, i)

                @block.gpsimd
                def _(e):
                    def rstd(b, _):
                        e.wait_ge(var_done, b + 1)
                        e.tensor_tensor(RSTD[:, :], VAR[:, :], MH[:, :], ALU.pow).then_inc(rstd_done, 1)

                    def low(b, t):
                        e.wait_ge(xh_done, CT * b + t + 1)
                        e.tensor_tensor(XL[:, t, :], SL[:, t, :] if L1 else X[:, b, t, :], XH[:, t, :].bitcast(F32),
                                        ALU.subtract).then_inc(xl_done, 1)

                    def qk_low(b, i):
                        e.wait_ge(hi_done, NQK * b + i + 1)
                        if L1:
                            hi, lo = [x[:, i % 2, :] for x in (keys, queries)[i // 2](b % 2)]
                            e.tensor_tensor(lo, SL[:, i % 2, :], hi.bitcast(F32), ALU.subtract).then_inc(lo_done, 1)
                        else:
                            p = 2 * K0
                            e.tensor_tensor(SL[0:p, 0, :].bitcast(F32R), SL[0:p, 0, :], SH[0:p, 0, :],
                                            ALU.subtract).then_inc(lo_done, 1)

                    def add(b, s):
                        h, j = s // NT, s % NT
                        e.wait_ge(exp_done, S * b + s + 1)
                        pa = PA[:, h * HALF:(h + 1) * HALF]
                        if j == 1:
                            if b:
                                e.wait_ge(d_full, index["sum", h, b - 1] + 1)
                        else:
                            e.wait_ge(sum_done, (NT - 1) * (2 * b + h) + j - 1)
                        e.tensor_tensor(pa, pr_slot(s - 1) if j == 1 else pa, pr_slot(s), ALU.add).then_inc(sum_done, 1)

                    for P in range(-1, B):
                        ev = []
                        if P >= 0:
                            ev += [(s, 2, add, P, s) for s in range(S) if s % NT]
                        if P + 1 < B:
                            at = {(u, i): a for a, u, i, b in plan[P] if b == P + 1}
                            if L1:
                                ev.append((0, 0, rstd, P + 1, 0))
                            ev += [(2 if L1 else 0, 1, low, P + 1, t) for t in range(CT)]
                            ev += [(at["qk", i] + 1 if P >= 0 else 3 + i, 3, qk_low, P + 1, i) for i in range(NQK)]
                        for _, _, f, b, i in sorted(ev, key=lambda x: (x[0], x[1], x[4])):
                            f(b, i)

                @block.sync
                def _(e):
                    for b in range(B):
                        if not L1:
                            e.wait_ge(lo_done, b + 1)
                            wait(e, st_full, S * (b - 1))
                            for dst, src in stack_copies(b % 2):
                                e.dma_start(dst, src).then_inc(stack_dma, 16)
                        e.wait_ge(d_free, index["T", 0, b] + 1)
                        if L1:
                            wait(e, st_full, S * b)
                            for i in range(2):
                                e.dma_start(MR1[i:i + 1, :], MRB[:, i, :]).then_inc(row_dma, 16)
                        else:
                            e.dma_start(QS[STACK:STACK + 1, b % 2, 0, :].bitcast(F32),
                                        MROW[0:NT, :].bitcast(F32)).then_inc(row_dma, 16)
                    e.wait_ge(row_dma, 16 * NROW * B)

        def stack_copies(slot):
            k, q = slice(0, K0), slice(K0, 2 * K0)
            for r, part in ((0, SH), (1, SL), (2, SH)):
                yield KS[r * K0:(r + 1) * K0, slot, 0, :].bitcast(F32), part[k, 0, :]
            for r, part in ((0, SH), (1, SH), (2, SL)):
                yield QS[r * K0:(r + 1) * K0, slot, 0, :].bitcast(F32), part[q, 0, :]

        def batch_norm():
            bn_var, bn_rstd = sem("bn_variance"), sem("bn_rstd")
            with nc.Block() as block:
                @block.vector
                def _(e):
                    for t in range(CT):
                        e.bn_aggr(MV[:, t, :], BNS[:, t].rearrange("p a b -> p (a b)"))
                    e.drain()
                    e.tensor_scalar(VAR[:, :], MV[:, :, 1], EPS, None, ALU.add).then_inc(bn_var, 1)
                    e.wait_ge(bn_rstd, 1)
                    norm_factors(e, 1, "bnw", "bnb")

                @block.gpsimd
                def _(e):
                    e.wait_ge(bn_var, 1)
                    e.tensor_tensor(RSTD[:, :], VAR[:, :], MH[:, :], ALU.pow).then_inc(bn_rstd, 1)

        ROUNDS = 2 * B
        NGRP = ROUNDS * GROUPS

        M_AT = (5.5, 58)
        HOLES = [[(35, 39)], [(12, 13.5), (35, 39)]]
        XN_AT = 12
        HALVES_AT = {"v": (0, 1), "w": (3.5, 5), "K": (28, 29.3), "Q": (30.6, 31.9), "p": (14.5, 17.5, 20.5, 23.5)}
        BANKS = 4

        def side_units(g, first):
            halves = dict(HALVES_AT)
            if g == 0 and first:
                halves |= {"s": (0, 0), "k": (0.5, 0.5), "q": (0.6, 0.6), "v": (1, 1), "w": (2, 2)}
            if g == 1:
                halves["s"] = (2.4, 2.4)
            if g == 0 or first:
                del halves["p"]
            units = [(u, at, i) for u, ats in halves.items() for i, at in enumerate(ats)]
            n = QUADH * NT * 2
            spacing = (M_AT[1] - M_AT[0] - sum(b - a for a, b in HOLES[g])) / n
            for i in range(n):
                at = M_AT[0] + i * spacing
                for a, b in HOLES[g]:
                    at += (b - a) * (at > a)
                units.append(("m", at, i))
            units.append(("T", M_AT[1] + 1.5, 0))
            return sorted(units, key=lambda x: x[1])

        def bank(place, k):
            i = (BASE["all"][place] + k) % BANKS
            return psD[:, i // 2, i % 2 * HALF:(i % 2 + 1) * HALF]

        def taken(units, k, engine):
            return sum((u in "vwkqKQ") == (engine == "scalar") for u, _, _ in units[:k])

        UNITS = [side_units(0, True), side_units(1, True), side_units(0, False), side_units(1, False)]
        BASE = {"all": [sum(len(u) for u in UNITS[:i]) for i in range(5)]}
        for _e in ("scalar", "vector"):
            BASE[_e] = [sum(taken(u, len(u), _e) for u in UNITS[:i]) for i in range(5)]
        LOOP = {k: v[4] - v[2] for k, v in BASE.items()}
        TAIL = {k: v[2] + LOOP[k] * (ROUNDS - 1) for k, v in BASE.items()}
        assert LOOP["all"] % BANKS == 0
        assert all("".join(x[0] for x in u[-BANKS:]) == "m" * (BANKS - 1) + "T" for u in UNITS)

        def base_of(kind, place, r):
            return BASE[kind][place] if r is None else r * LOOP[kind] + BASE[kind][place]

        def units_taken(G, u):
            place, r = (G, None) if G < 2 else (2 + G % 2, G // 2 - 1)
            units = UNITS[place]
            return base_of("vector", place, r) + taken(units, [x[0] for x in units].index(u) + 1, "vector")

        WEIGH = [("av", 0, 12), ("av", 1, 13), ("av", 2, 15), ("av", 3, 18), ("av", 4, 22), ("av", 5, 26),
                 ("av", 6, 28), ("sum", 6, 30), ("av", 7, 33), ("sum", 7, 34), ("pa", NT, 35)]
        LAST_PIECES = [("av", j) for j in range(NT - DIRECT)] + [("sum", j) for j in range(NT - DIRECT, NT - 1)] + [("pa", NT)]
        assert [j for kind, j, _ in WEIGH if kind == "sum"] == list(range(NT - DIRECT, NT))
        HALF_STEPS = STEPS // 2
        TAKE_AT = 35.9

        def all_phases(e, phase):
            def two_phases(r, even, odd, proj, norm_b):
                phase(r * 2 + 1, 1, r * 2 + 2, 0, 2, r, even)
                phase(r * 2 + 2, 0, r * 2 + 3, 1, 3, r, odd, proj=proj, norm=r + 2, norm_b=norm_b)

            two, three = (2, 2, 2, 2), (3, 3, 3, 3)
            phase(None, None, 0, 0, 0, None, two, norm=0, norm_b=0)
            phase(0, 0, 1, 1, 1, None, two, norm=1, norm_b=1)
            with e.Fori(0, B - 2) as r:
                two_phases(r, two, two, r, r + 2)
            two_phases(B - 2, two, (2, 3, 3, 2), B - 2, 0)
            two_phases(B - 1, three, (3, 3, 3, 2), B - 1, 1)
            with e.Fori(B, ROUNDS - 1) as r:
                two_phases(r, three, three, r - B, (r + 2) % B)
            phase(NGRP - 1, 1, None, None, 4, None, three)

        def eight_heads():
            split_weights(2)
            scale = CH ** -0.5
            n = "_23"
            w3_staged = SH[:, :, :].rearrange("p t n -> p (t n)")[:, 0:CT * 3 * C].rearrange("p (t n) -> p t n", t=CT)
            w3_loaded, w3_high, w3_split = sem("w3_loaded"), sem("w3_high"), sem("w3_split")
            d_full = sem("unit_full" + n)
            vec_free, act_free = sem("unit_taken_by_vector" + n), sem("unit_taken_by_scalar" + n)
            st_full, exp_done = sem("scores_full" + n), sem("exp_done" + n)
            av_done, sum_done, out_done = sem("av_done" + n), sem("sum_done" + n), sem("out_done" + n)
            stat_done, var_done, rstd_done = sem("stat_done" + n), sem("var_done" + n), sem("rstd_done" + n)
            xn_done, xh_done, xl_done = sem("xn_done" + n), sem("xh_done" + n), sem("xl_done" + n)
            high_done, low_done, row_dma = sem("qk_high" + n), sem("qk_low" + n), sem("max_row_filled" + n)
            stack_dma = [sem(f"stack_filled{n}_head{q}") for q in range(QUADH)]
            s_out = sem("stored" + n)

            def stacks_filled(e, G, heads=range(QUADH)):
                for q in heads:
                    wait(e, stack_dma[q], (G + 1) * STACK_DMAS * 16)

            def units_full(G, u):
                names = [x[0] for x in UNITS[2 + G % 2]]
                return base_of("all", 2 + G % 2, G // 2 - 1) + len(names) - names[::-1].index(u)

            with nc.Block() as block:
                @block.tensor
                def _(e):
                    def weigh(P, p, h, kind, j):
                        if kind == "pa":
                            wait(e, sum_done, ADDS * (2 * P + h + 1))
                        elif kind == "av":
                            if j == 0:
                                wait(e, out_done, 2 * P + h)
                            wait(e, exp_done, STEPS * P + QUADH * (NT * h + j + 1))
                        source = PA[:, :] if kind == "pa" else PR[:, j % 4, :]
                        source = source.rearrange("p (q n) -> p q n", q=QUADH)
                        for q in range(QUADH):
                            cols = slice(CH * q, CH * q + CH)
                            if kind == "av":
                                mm = e.matmul(psO[cols, 0, :], V[:, p, j, cols], source[:, q, :],
                                              start=(j == 0), stop=(j == NT - 1))
                            else:
                                mm = e.matmul(psO[cols, 1, :], ones[:, 0:CH], source[:, q, :],
                                              start=(j == NT - DIRECT), stop=(j == NT))
                        if (kind, j) in LAST_PIECES:
                            mm.then_inc(av_done, 1)

                    def all_taken(place, r, k):
                        engine = "scalar" if k > 0 and UNITS[place][k - 1][0] in "vwkqKQ" else "vector"
                        count = min(k, 0) + taken(UNITS[place], max(k, 0), engine)
                        wait(e, act_free if engine == "scalar" else vec_free, base_of(engine, place, r) + count)

                    def project(out_ap, column, h):
                        mv = slice(h * HALF, (h + 1) * HALF)
                        return split_products(e, out_ap, [(w[:, t, column:column + PART], xx[:, t, mv])
                                                          for w, xx in ((WH, XH), (WL, XH), (WH, XL)) for t in range(CT)])

                    def output(out_ap, i, group_halves, layer):
                        o, mv = slice(i // 2 * PART, (i // 2 + 1) * PART), slice(i % 2 * HALF, (i % 2 + 1) * HALF)
                        wait(e, out_done, group_halves)
                        e.wait_ge(wp_loaded[layer], 16)
                        return split_products(e, out_ap, [(WP[:, t, o], A[:, t, mv]) for t in range(CT)])

                    def unit(place, r, k, G, g, t, layers):
                        u, _, i = UNITS[place][k]
                        full = bank(place, k)
                        if place or k >= BANKS:
                            all_taken(place, r, k - BANKS + 1)
                        if u == "s":
                            wait(e, stat_done, t + 1)
                            mm = e.matmul(full[:, 0:2], gmat[:, :], GST[:, i, :], start=True, stop=True)
                        elif u in "kqKQ":
                            group, gg = (G, g) if u in "kq" else (G + 1, 1 - g)
                            if u in "kK" and i == 0:
                                wait(e, xh_done, group - gg + CT)
                                wait(e, xl_done, group - gg + CT)
                                if layers[1] == 3:
                                    e.wait_ge(w3_split, 1)
                            mm = project(full, 2 * PART * gg + PART * (u in "qQ"), i)
                        elif u == "v":
                            mm = project(full, 2 * C + PART * g, i)
                        elif u == "w":
                            all_taken(place, r, k)
                            for n in range(NT // 2):
                                st = slice(i * HALF + n * PART, i * HALF + (n + 1) * PART)
                                mm = e.transpose(full[:, n * PART:(n + 1) * PART], VT[:, st], ident[:, :])
                        elif u == "m":
                            q, tile, h = i // (2 * NT), i // 2 % NT, i % 2
                            if i % (2 * NT) == 0:
                                stacks_filled(e, G, [q])
                            mm = e.matmul(full, QS[0:STACK, g, q, tile * PART:(tile + 1) * PART],
                                          KS[0:STACK, g, q, h * HALF:(h + 1) * HALF], start=True, stop=True)
                        elif u == "T":
                            all_taken(place, r, k)
                            mm = e.transpose(full[0:QUADH * NT, 0:PART], MX[:, :], ident[:, :])
                        else:
                            mm = output(full, i, t, layers[3])
                        mm.then_inc(d_full, 1)

                    def phase(P, p, G, g, place, r, layers, proj=None, norm=None, norm_b=None):
                        todo = [] if G is None else [(at, k) for k, (_, at, _) in enumerate(UNITS[place])]

                        def next_unit():
                            k = todo.pop(0)[1]
                            unit(place, r, k, G, g, norm if UNITS[place][k][0] == "s" else None if P is None else P * 2,
                                 layers)

                        if P is None:
                            while todo:
                                next_unit()
                            return
                        wait(e, row_dma, (P + 1) * 16)
                        for s in range(STEPS):
                            h, j, q = s // (NT * QUADH), s // QUADH % NT, s % QUADH
                            wait(e, exp_done, STEPS * P + s - 1)
                            e.matmul(psA[:, s % 2, :], KS[0:STACK + 1, p, q, j * PART:(j + 1) * PART],
                                     QS[0:STACK + 1, p, q, h * HALF:(h + 1) * HALF],
                                     start=True, stop=True).then_inc(st_full, 1)
                            while todo and todo[0][0] <= s:
                                next_unit()
                            for kind, j, at in WEIGH:
                                if at + HALF_STEPS - STEPS == s and not (isinstance(P, int) and P == 0):
                                    weigh(P - 1, 1 - p, 1, kind, j)
                                for h in range(2):
                                    if at + HALF_STEPS * h == s:
                                        weigh(P, p, h, kind, j)

                    def tail():
                        for kind, j, at in WEIGH:
                            if at + HALF_STEPS >= STEPS:
                                weigh(NGRP - 1, 1, 1, kind, j)
                        for i in range(2 * CT):
                            e.wait_ge(vec_free, TAIL["vector"] - BANKS + 1 + i)
                            output(bank(4, i), i, 2 * NGRP, 3).then_inc(d_full, 1)

                    all_phases(e, phase)
                    tail()

                @block.vector
                def _(e):
                    def take_half(P, p, h):
                        wait(e, av_done, (2 * P + h + 1) * NT)
                        out_ap = A[:, p, h * HALF:(h + 1) * HALF]
                        e.reciprocal(out_ap, psO[:, 1, :])
                        e.drain()
                        e.tensor_tensor(out_ap, psO[:, 0, :], out_ap, ALU.mult).then_inc(out_done, 1)

                    def batch(b):
                        return X[:, b] if isinstance(b, int) else X[:, bass.ds(b, 1)].rearrange("p b t n -> p (b t) n")

                    def factors(b):
                        return SC[:, b] if isinstance(b, int) else SC[:, bass.ds(b, 1)].rearrange("p b t n -> p (b t) n")

                    def add_residual(i, b, full, layer):
                        c = i // 2
                        xb, sc = batch(b)[:, c, i % 2 * HALF:(i % 2 + 1) * HALF], factors(b)
                        if layer == 2:
                            e.tensor_scalar(xb, xb, sc[:, c, 0:1], sc[:, c, 1:2], ALU.mult, ALU.add)
                            e.drain()
                        return e.scalar_tensor_tensor(out=xb, in0=full, scalar=par(f"bp{layer}", 2)[:, c:c + 1],
                                                      in1=xb, op0=ALU.add, op1=ALU.add)

                    def normalise(norm, b, P, G, layer):
                        e.wait_ge(rstd_done, norm + 1)
                        norm_factors_at(b, layer)
                        if P is not None:
                            stacks_filled(e, G)
                        xb, sc = batch(b), factors(b)
                        for c in range(CT):
                            e.tensor_scalar(SL[:, c, :], xb[:, c, :], sc[:, c, 0:1], sc[:, c, 1:2],
                                            ALU.mult, ALU.add).then_inc(xn_done, 1)

                    def take(place, r, k, G, g, proj, layers):
                        u, _, i = UNITS[place][k]
                        e.wait_ge(d_full, base_of("all", place, r) + k + 1)
                        full = bank(place, k)
                        if u == "s":
                            e.tensor_copy(MV[:, i, :], full[:, 0:2]).then_inc(vec_free, 1)
                            if i == 1:
                                group_variance(e).then_inc(var_done, 1)
                        elif u == "m":
                            q, tile, h = i // (2 * NT), i // 2 % NT, i % 2
                            top = e.tensor_reduce(MXH[:, h, q, tile:tile + 1], full, AX.X, ALU.max)
                            if i == 2 * QUADH * NT - 1:
                                e.drain()
                                top = e.tensor_tensor(MX[:, :].rearrange("p (q t) -> p q t", q=QUADH), MXH[:, 0], MXH[:, 1],
                                                      ALU.max)
                            top.then_inc(vec_free, 1)
                        elif u == "T":
                            wait(e, row_dma, G * 16)
                            e.tensor_scalar(MROW[:, :], full[0:QUADH * NT, 0:PART], -1.0, None,
                                            ALU.mult).then_inc(vec_free, 1)
                        else:
                            add_residual(i, proj, full, layers[3]).then_inc(vec_free, 1)

                    def split_next_weights():
                        e.wait_ge(w3_loaded, 16)
                        e.wait_ge(d_full, units_full(NGRP // 2 - 1, "v"))
                        e.tensor_copy(WH[:, :, :], w3_staged).then_inc(w3_high, 1)
                        e.wait_ge(w3_high, 1)
                        e.tensor_tensor(WL[:, :, :], w3_staged, WH[:, :, :].bitcast(F32),
                                        ALU.subtract).then_inc(w3_split, 1)

                    def phase(P, p, G, g, place, r, layers, proj=None, norm=None, norm_b=None):
                        events = [(at, 0, k, "unit") for k, (u, at, i) in enumerate([] if G is None else UNITS[place])
                                  if u not in "vwkqKQ"]
                        if norm is not None:
                            events.append((-1, 0, 0, "stats"))
                            events.append((0.2 if P is None else XN_AT, 0, 0, "xn"))
                        if layers[0] != layers[1]:
                            events.append((XN_AT + 0.1, 0, 0, "weights"))
                        if P is not None:
                            if not (isinstance(P, int) and P == 0):
                                events.append((TAKE_AT - HALF_STEPS, 0, 1, "half before"))
                            events.append((TAKE_AT, 0, 0, "half"))
                        for _, _, k, what in sorted(events):
                            if what == "half before":
                                take_half(P - 1, 1 - p, 1)
                            elif what == "half":
                                take_half(P, p, 0)
                            elif what == "weights":
                                split_next_weights()
                            elif what == "stats":
                                norm_statistics(e, batch(norm_b)).then_inc(stat_done, 1)
                            elif what == "xn":
                                normalise(norm, norm_b, P, G, layers[2])
                            else:
                                take(place, r, k, G, g, proj, layers)

                    def norm_factors_at(b, layer):
                        sc = factors(b)
                        e.tensor_tensor(sc[:, :, 0], RSTD[:, :], par(f"gw{layer}", 2), ALU.mult)
                        e.drain()
                        e.tensor_tensor(TMP[:, :], MV[:, :, 0], sc[:, :, 0], ALU.mult)
                        e.drain()
                        e.tensor_tensor(sc[:, :, 1], par(f"gb{layer}", 2), TMP[:, :], ALU.subtract)
                        e.drain()

                    all_phases(e, phase)
                    take_half(NGRP - 1, 1, 1)
                    for i in range(2 * CT):
                        e.wait_ge(d_full, TAIL["all"] + i + 1)
                        add_residual(i, B - 1, bank(4, i), 3).then_inc(vec_free, 1)
                    e.drain()

                @block.scalar
                def _(e):
                    def run(what, k, place, r, G, g, norm, layers):
                        if what == "x":
                            c = k
                            e.wait_ge(xn_done, CT * norm + c + 1)
                            if place:
                                used = [u for u, _, _ in UNITS[place]].index("v") + 1
                                e.wait_ge(d_full, base_of("all", place, r) + used)
                            e.activation(XH[:, c, :], SL[:, c, :], ACT.Copy).then_inc(xh_done, 1)
                            return
                        u, _, i = UNITS[place][k]
                        group, gg = (G + 1, 1 - g) if u in "KQ" else (G, g)
                        which, mv = int(u in "qQ"), slice(i * HALF, (i + 1) * HALF)
                        if what == "high":
                            e.drain()
                            e.activation(SH[:, which, :].bitcast(F32R), SL[:, which, :], ACT.Copy).then_inc(high_done, 1)
                            return
                        full = bank(place, k)
                        e.wait_ge(d_full, base_of("all", place, r) + k + 1)
                        if u == "w":
                            wait(e, av_done, (G - 1) * 2 * NT)
                            e.activation(V[:, g, i * NT // 2:(i + 1) * NT // 2, :].rearrange("p t c -> p (t c)"), full,
                                         ACT.Copy).then_inc(act_free, 1)
                        else:
                            if u == "K" and i == 0:
                                stacks_filled(e, G)
                            bias = (par(f"bv{layers[0]}", 2)[:, g:g + 1] if u == "v"
                                    else par(f"bqk{layers[1]}", 4)[:, 2 * gg + which:2 * gg + which + 1])
                            e.activation(VT[:, mv] if u == "v" else SL[:, which, mv], full, ACT.Identity,
                                         bias=bias).then_inc(act_free, 1)

                    def phase(P, p, G, g, place, r, layers, proj=None, norm=None, norm_b=None):
                        events = []
                        for k, (u, at, i) in enumerate([] if G is None else UNITS[place]):
                            if u in "vwkqKQ":
                                step = -int(-at // 1) + 1
                                if P is not None:
                                    assert -int(-UNITS[place][k + BANKS][1] // 1) >= step
                                events.append((step, 0, "unit", k))
                                if i == 1 and u in "kqKQ":
                                    events.append((step + 1 if P is not None else step, 1, "high", k))
                        if norm is not None:
                            events += [(-1 if P is None else XN_AT + 3 + 2 * c, 0, "x", c) for c in range(CT)]
                        events.sort()

                        if P is None:
                            for x in events:
                                run(*x[2:], place, r, G, g, norm, layers)
                            return
                        for s in range(STEPS):
                            J = s // QUADH
                            if s % QUADH == 0:
                                if J >= 4:
                                    wait(e, av_done, 2 * NT * P + J - 3)
                                    h, j = (J - 4) // NT, (J - 4) % NT
                                    wait(e, sum_done, ADDS * (2 * P + h) + min(max(j, 1), ADDS))
                                else:
                                    wait(e, av_done, 2 * NT * P + J - 3)
                                    wait(e, sum_done, ADDS * 2 * P)
                            wait(e, st_full, STEPS * P + s + 1)
                            e.activation(PR[:, J % 4, (s % QUADH) * HALF:(s % QUADH + 1) * HALF], psA[:, s % 2, :],
                                         ACT.Exp, scale=scale).then_inc(exp_done, 1)
                            while events and events[0][0] <= s:
                                run(*events.pop(0)[2:], place, r, G, g, norm, layers)

                    all_phases(e, phase)

                @block.gpsimd
                def _(e):
                    def rstd(norm):
                        e.wait_ge(var_done, norm + 1)
                        e.tensor_tensor(RSTD[:, :], VAR[:, :], MH[:, :], ALU.pow).then_inc(rstd_done, 1)

                    def input_low(norm):
                        for c in range(CT):
                            e.wait_ge(xh_done, CT * norm + c + 1)
                            e.tensor_tensor(XL[:, c, :], SL[:, c, :], XH[:, c, :].bitcast(F32),
                                            ALU.subtract).then_inc(xl_done, 1)

                    def low(group, which):
                        wait(e, high_done, group * 2 + which + 1)
                        e.tensor_tensor(SL[:, which, :].bitcast(F32R), SL[:, which, :], SH[:, which, :],
                                        ALU.subtract).then_inc(low_done, 1)

                    def phase(P, p, G, g, place, r, layers, proj=None, norm=None, norm_b=None):
                        if P is None:
                            rstd(norm)
                            input_low(norm)
                            for which in range(4):
                                low(which // 2, which % 2)
                            return
                        elif norm is not None:
                            rstd(norm)
                        for h in range(2):
                            for j in range(1, ADDS + 1):
                                J = h * NT + j
                                wait(e, exp_done, STEPS * P + QUADH * (J + 1))
                                if j == 1:
                                    wait(e, av_done, NT * (2 * P + h))
                                else:
                                    wait(e, sum_done, ADDS * (2 * P + h) + j - 1)
                                e.tensor_tensor(PA[:, :], PR[:, (J - 1) % 4, :] if j == 1 else PA[:, :],
                                                PR[:, J % 4, :], ALU.add).then_inc(sum_done, 1)
                                if norm is not None and h == 0 and j == 3:
                                    input_low(norm)
                            if G is not None and h == 0:
                                for which in range(2):
                                    low(G + 1, which)

                    all_phases(e, phase)

                @block.sync
                def _(e):
                    for G in range(NGRP):
                        g = G % 2
                        e.wait_ge(low_done, 2 * (G + 1))
                        wait(e, st_full, STEPS * (G - 1))
                        for q in range(QUADH):
                            rows = slice(CH * q, CH * (q + 1))
                            for r in range(3):
                                dst = slice(CH * r, CH * (r + 1))
                                e.dma_start(KS[dst, g, q, :].bitcast(F32),
                                            (SH, SL, SH)[r][rows, 0, :]).then_inc(stack_dma[q], 16)
                                e.dma_start(QS[dst, g, q, :].bitcast(F32),
                                            (SH, SH, SL)[r][rows, 1, :]).then_inc(stack_dma[q], 16)
                        if G == NGRP // 2 - 1:
                            stacks_filled(e, G)
                            e.dma_start(w3_staged, w_dram[3]).then_inc(w3_loaded, 16)
                        if G == NGRP // 2 + 1:
                            e.wait_ge(d_full, units_full(G, "p"))
                            e.dma_start(WP[:, :, :], wp_dram[3]).then_inc(wp_loaded[3], 16)
                        b = G // 2 - 2 - B
                        if g == 0 and b >= 0:
                            e.dma_start(out_v[:, b], X[:, b]).then_inc(s_out, 16)
                        e.wait_ge(vec_free, units_taken(G, "T"))
                        e.dma_start(QS[STACK:STACK + 1, g, :, :].rearrange("p q n -> p (q n)").bitcast(F32),
                                    MROW[:, :].bitcast(F32)).then_inc(row_dma, 16)
                    e.dma_start(out_v[:, B - 2], X[:, B - 2]).then_inc(s_out, 16)
                    e.wait_ge(vec_free, TAIL["vector"] + 2 * CT)
                    e.dma_start(out_v[:, B - 1], X[:, B - 1]).then_inc(s_out, 16)
                    e.wait_ge(s_out, 16 * B)

        single_head(0)
        batch_norm()
        single_head(1)
        eight_heads()


def laid_out(inputs):
    import numpy as np

    f = {k: np.asarray(v) for k, v in inputs.items()}
    ident = np.eye(PART, dtype=np.float32)
    gmat = np.kron(np.eye(PART // 8), np.full((8, 8), 1 / 8)).astype(np.float32)
    par = np.zeros((PART, NPAR), np.float32)

    def put(name, v):
        v = np.asarray(v).reshape(-1)
        for i in range(max(1, len(v) // PART)):
            w = v[i * PART:(i + 1) * PART]
            par[:len(w), PC[name] + i] = w

    par[:, PC["gamma0"]] = f["L0_conv_gamma"]
    put("bnw", f["L0_conv_bn_w"])
    put("bnb", f["L0_conv_bn_b"])
    put("bqk0", np.concatenate([f["L0_conv_bk"], f["L0_conv_bq"]]))
    w, bv, wp = [], [], []
    w.append(np.concatenate([f["L0_conv_Wk"], f["L0_conv_Wq"], f["L0_conv_Wv"]]))
    bv.append(f["L0_conv_bv"])
    order = np.concatenate([np.arange(C, 2 * C), np.arange(C), np.arange(2 * C, 3 * C)])
    orders = {1: order}
    rows = np.arange(3 * C).reshape(HEADS, 3, CH)
    parts = [rows[g * QUADH:(g + 1) * QUADH, k].reshape(-1) for g in range(GROUPS) for k in (1, 0)]
    orders[2] = orders[3] = np.concatenate(parts + [rows[:, 2].reshape(-1)])
    norm = {1: ("gamma", "beta"), 2: ("gn_w", "gn_b"), 3: ("norm_scale", "norm_bias")}
    for n in (1, 2, 3):
        pre = f"L{n}_conv_"
        wl, bl = f[pre + "qkv_w"][orders[n]], f[pre + "qkv_b"][orders[n]]
        w.append(wl)
        bv.append(bl[2 * C:])
        wp.append(f[pre + "proj_w"])
        put(f"gw{n}", f[pre + norm[n][0]])
        put(f"gb{n}", f[pre + norm[n][1]])
        put(f"bp{n}", f[pre + "proj_b"])
        put(f"bv{n}", bl[2 * C:])
        put(f"bqk{n}", bl[:2 * C])
    arrays = {"x": np.ascontiguousarray(f["x"].reshape(B, C, N))}
    for n in range(4):
        arrays[f"w{n}"] = np.ascontiguousarray(w[n].T)
    for n in (1, 2, 3):
        arrays[f"wp{n}"] = np.ascontiguousarray(wp[n - 1].T)
    for n in range(2):
        arrays[f"bv{n}"] = np.ascontiguousarray(np.broadcast_to(bv[n], (PART, C)))
    arrays |= {"par": par, "ident": ident, "gmat": gmat}
    return arrays


def kernel(**inputs):
    import concourse.bacc as bacc
    from concourse.bass_utils import run_bass_kernel_spmd

    nc = bacc.Bacc("TRN2", target_bir_lowering=False, num_devices=1)
    arrays = laid_out(inputs)
    args = [nc.dram_tensor(k, a.shape, mybir.dt.from_np(a.dtype), kind="ExternalInput").ap() for k, a in arrays.items()]
    args.append(nc.dram_tensor("out", (B, C, N), F32, kind="ExternalOutput").ap())
    attention_stack(nc, *args)
    r = run_bass_kernel_spmd(nc, [arrays], core_ids=[0])
    return r.results[0]["out"].reshape(B, C, 32, 32)
```
